# Optimizing a Trainium2 kernel written in Bass

```python
import numpy as np
import jax
import jax.numpy as jnp

def _softmax(x, axis=-1):
    return jax.nn.softmax(x, axis=axis)

def _gelu(x):
    return jax.nn.gelu(x, approximate=True)

def _silu(x):
    return jax.nn.silu(x)

def _sigmoid(x):
    return jax.nn.sigmoid(x)

def _layernorm(x, axis=-1, eps=1e-05):
    m = jnp.mean(x, axis=axis, keepdims=True)
    v = jnp.var(x, axis=axis, keepdims=True)
    return (x - m) / jnp.sqrt(v + eps)

def _scatter_add(tgt, idx, src, axis=0):
    return tgt.at[idx].add(src)

def _segment_sum(src, seg, n):
    return jax.ops.segment_sum(src, seg, n)
kernel_name = 'mk_adaln_attn_ffn_d1_seqx_r8_363b51'

def setup_inputs(seed: int=0):
    np.random.seed(seed)
    _w = jnp.asarray

    def _rec_inputs():
        import jax
        import jax.numpy as jnp
        _rk = jax.random.key(seed)
        x = -7.109e-05 + 0.9999 * jax.random.normal(jax.random.fold_in(_rk, 1), (128, 32, 256), jnp.float32)
        _lenS = 32 - jax.random.randint(jax.random.fold_in(_rk, 7), (128,), 0, max(1, 32 // 4) + 1, jnp.int32)
        _lenS2 = 32 - jax.random.randint(jax.random.fold_in(_rk, 8), (128,), 0, max(1, 32 // 4) + 1, jnp.int32)
        itok_B_1_198 = jax.random.randint(jax.random.fold_in(_rk, 11), (128,), 1, 199, jnp.int32)
        itok_B_0_6 = jax.random.randint(jax.random.fold_in(_rk, 12), (128,), 0, 7, jnp.int32)
        return (x, itok_B_1_198, itok_B_0_6)
    x, itok_B_1_198, itok_B_0_6 = _rec_inputs()

    def _L0_cond_setup():
        import jax, jax.numpy as jnp
        import numpy as np
        B, C, T = (128, 32, 256)
        S, D = (200, 32)
        key = jax.random.key(seed)
        k1, k2, k3 = jax.random.split(key, 3)
        x = jax.random.normal(k1, (B, C, T), dtype=jnp.float32)
        conditions = jax.random.randint(k2, (B,), 0, S, dtype=jnp.int64)
        weights = jax.random.normal(k3, (S, C, D), dtype=jnp.float32) / jnp.sqrt(jnp.float32(C))
        return {'x': x, 'conditions': conditions, 'weights': weights}
    _L0_cond_all = _L0_cond_setup()
    _L0_cond_in = {k: v for k, v in _L0_cond_all.items() if k in ('weights',)}
    del _L0_cond_all

    def _L0_attn_setup():
        import jax, jax.numpy as jnp
        import numpy as np
        HIDDEN = 256
        NKH, NVH, HD, K = (16, 32, 128, 4)
        KDIM = NKH * HD
        VDIM = NVH * HD
        CONV = 2 * KDIM + VDIM
        EXP = NVH // NKH

        def _l2norm(a):
            n = jnp.sqrt(jnp.sum(a * a, axis=-1, keepdims=True))
            return a / jnp.maximum(n, 1e-12)

        def _reference_tuple_inner(x, W_qkv, W_z, W_b, W_a, conv_w, dt_bias, A_log, norm_w, W_out):
            B, T, _ = x.shape
            qkv = jnp.einsum('bth,ch->btc', x, W_qkv)
            z = jnp.einsum('bth,vh->btv', x, W_z)
            b_raw = jnp.einsum('bth,nh->btn', x, W_b)
            a_raw = jnp.einsum('bth,nh->btn', x, W_a)
            qkv_t = jnp.swapaxes(qkv, 1, 2)
            padded = jnp.concatenate([jnp.zeros((B, CONV, K - 1), x.dtype), qkv_t], axis=2)
            w = conv_w[:, 0, :]
            conv = sum((w[None, :, j:j + 1] * padded[:, :, j:j + T] for j in range(K)))
            conv = jax.nn.silu(conv)
            new_conv_buf = padded[..., T:]
            qkvc = jnp.swapaxes(conv, 1, 2)
            q = qkvc[..., :KDIM].reshape(B, T, NKH, HD)
            kk = qkvc[..., KDIM:2 * KDIM].reshape(B, T, NKH, HD)
            v = qkvc[..., 2 * KDIM:].reshape(B, T, NVH, HD)
            q = jnp.repeat(q, EXP, axis=2)
            kk = jnp.repeat(kk, EXP, axis=2)
            q = _l2norm(q)
            kk = _l2norm(kk)
            beta = jax.nn.sigmoid(b_raw)
            g = -jnp.exp(A_log) * jax.nn.softplus(a_raw + dt_bias)
            decay = jnp.exp(g)
            state0 = jnp.zeros((B, NVH, HD, HD), x.dtype)
            tm = lambda a: jnp.moveaxis(a, 1, 0)

            def step(state, inp):
                q_t, k_t, v_t, b_t, d_t = inp
                state = state * d_t[..., None, None]
                Sk = jnp.einsum('bhi,bhij->bhj', k_t, state)
                delta = (v_t - Sk) * b_t[..., None]
                state = state + jnp.einsum('bhi,bhj->bhij', k_t, delta)
                o = jnp.einsum('bhi,bhij->bhj', q_t, state)
                return (state, o)
            state, o = jax.lax.scan(step, state0, (tm(q), tm(kk), tm(v), tm(beta), tm(decay)))
            o = jnp.moveaxis(o, 0, 1)
            zz = z.reshape(B, T, NVH, HD)
            y = o * jax.nn.silu(zz)
            y = y * jax.lax.rsqrt(jnp.mean(y * y, axis=-1, keepdims=True) + 1e-06) * norm_w
            out = jnp.einsum('btv,ov->bto', y.reshape(B, T, VDIM), W_out)
            return (out, state, new_conv_buf)
        key = jax.random.key(seed)
        ks = jax.random.split(key, 8)
        s = 0.02
        B, T = (2, 256)
        return {'x': jax.random.normal(ks[0], (B, T, HIDDEN), jnp.float32), 'W_qkv': jax.random.normal(ks[1], (CONV, HIDDEN), jnp.float32) * s, 'W_z': jax.random.normal(ks[2], (VDIM, HIDDEN), jnp.float32) * s, 'W_b': jax.random.normal(ks[3], (NVH, HIDDEN), jnp.float32) * s, 'W_a': jax.random.normal(ks[4], (NVH, HIDDEN), jnp.float32) * s, 'conv_w': jax.random.normal(ks[5], (CONV, 1, K), jnp.float32) * 0.1, 'dt_bias': jnp.ones((NVH,), jnp.float32), 'A_log': jnp.zeros((NVH,), jnp.float32), 'norm_w': jnp.ones((HD,), jnp.float32), 'W_out': jax.random.normal(ks[6], (HIDDEN, VDIM), jnp.float32) * s}
    _L0_attn_all = _L0_attn_setup()
    _L0_attn_in = {k: v for k, v in _L0_attn_all.items() if k in ('W_qkv', 'W_z', 'W_b', 'W_a', 'conv_w', 'dt_bias', 'A_log', 'norm_w', 'W_out')}
    del _L0_attn_all

    def _L0_cond2_setup():
        import jax, jax.numpy as jnp
        import numpy as np
        B, T, D_IN, D_OUT = (16, 256, 256, 256)
        N_ADAPTERS, RANK = (8, 16)
        key = jax.random.key(seed)
        k_x, k_w, k_a, k_b, k_s, k_idx = jax.random.split(key, 6)
        x = jax.random.normal(k_x, (B, T, D_IN), dtype=jnp.float32)
        W = jax.random.normal(k_w, (D_OUT, D_IN), dtype=jnp.float32) * (1.0 / np.sqrt(D_IN))
        A = jax.random.normal(k_a, (N_ADAPTERS, RANK, D_IN), dtype=jnp.float32) * 0.02
        Bm = jax.random.normal(k_b, (N_ADAPTERS, D_OUT, RANK), dtype=jnp.float32) * 0.02
        scalings = jnp.ones((N_ADAPTERS,), dtype=jnp.float32)
        adapter_idx = jax.random.randint(k_idx, (B,), 0, N_ADAPTERS, dtype=jnp.int32)
        return {'x': x, 'W': W, 'A': A, 'Bm': Bm, 'scalings': scalings, 'adapter_idx': adapter_idx}
    _L0_cond2_all = _L0_cond2_setup()
    _L0_cond2_in = {k: v for k, v in _L0_cond2_all.items() if k in ('W', 'A', 'Bm', 'scalings')}
    del _L0_cond2_all

    def _L0_ffn_setup():
        import jax, jax.numpy as jnp
        import numpy as np
        B, S, D, H = (4, 256, 256, 1024)

        def fwht(x):
            orig_shape = x.shape
            n = orig_shape[-1]
            x = x.reshape(-1, n)
            h = 1
            while h < n:
                xb = x.reshape(-1, n // (2 * h), 2, h)
                a = xb[:, :, 0, :]
                b = xb[:, :, 1, :]
                x = jnp.stack([a + b, a - b], axis=2).reshape(-1, n)
                h *= 2
            scale = jnp.asarray(1.0 / np.sqrt(n), dtype=x.dtype)
            return (x * scale).reshape(orig_shape)
        key = jax.random.key(seed)
        kx, k1, k2, k3 = jax.random.split(key, 4)
        x = jax.random.normal(kx, (B, S, D), dtype=jnp.float32)
        W1 = jax.random.normal(k1, (H, D), dtype=jnp.float32) * (1.0 / np.sqrt(D))
        W2 = jax.random.normal(k2, (D, H), dtype=jnp.float32) * (1.0 / np.sqrt(H))
        W3 = jax.random.normal(k3, (H, D), dtype=jnp.float32) * (1.0 / np.sqrt(D))
        return {'x': x, 'W1': W1, 'W2': W2, 'W3': W3}
    _L0_ffn_all = _L0_ffn_setup()
    _L0_ffn_in = {k: v for k, v in _L0_ffn_all.items() if k in ('W1', 'W2', 'W3')}
    del _L0_ffn_all
    return {'x': x, 'itok_B_1_198': itok_B_1_198, 'itok_B_0_6': itok_B_0_6, 'L0_cond_weights': _L0_cond_in['weights'], 'L0_attn_W_qkv': _L0_attn_in['W_qkv'], 'L0_attn_W_z': _L0_attn_in['W_z'], 'L0_attn_W_b': _L0_attn_in['W_b'], 'L0_attn_W_a': _L0_attn_in['W_a'], 'L0_attn_conv_w': _L0_attn_in['conv_w'], 'L0_attn_dt_bias': _L0_attn_in['dt_bias'], 'L0_attn_A_log': _L0_attn_in['A_log'], 'L0_attn_norm_w': _L0_attn_in['norm_w'], 'L0_attn_W_out': _L0_attn_in['W_out'], 'L0_cond2_W': _L0_cond2_in['W'], 'L0_cond2_A': _L0_cond2_in['A'], 'L0_cond2_Bm': _L0_cond2_in['Bm'], 'L0_cond2_scalings': _L0_cond2_in['scalings'], 'L0_ffn_W1': _L0_ffn_in['W1'], 'L0_ffn_W2': _L0_ffn_in['W2'], 'L0_ffn_W3': _L0_ffn_in['W3']}

def reference(x, itok_B_1_198, itok_B_0_6, L0_cond_weights, L0_attn_W_qkv, L0_attn_W_z, L0_attn_W_b, L0_attn_W_a, L0_attn_conv_w, L0_attn_dt_bias, L0_attn_A_log, L0_attn_norm_w, L0_attn_W_out, L0_cond2_W, L0_cond2_A, L0_cond2_Bm, L0_cond2_scalings, L0_ffn_W1, L0_ffn_W2, L0_ffn_W3):
    import jax
    import jax.numpy as jnp

    def _L0_cond_ref(x, conditions, weights):
        import jax, jax.numpy as jnp
        import numpy as np
        B, C, T = (128, 32, 256)
        S, D = (200, 32)
        w = weights[conditions]
        return jnp.einsum('bct,bcd->bdt', x, w)

    def _L0_attn_ref(x, W_qkv, W_z, W_b, W_a, conv_w, dt_bias, A_log, norm_w, W_out):
        import jax, jax.numpy as jnp
        import numpy as np
        HIDDEN = 256
        NKH, NVH, HD, K = (16, 32, 128, 4)
        KDIM = NKH * HD
        VDIM = NVH * HD
        CONV = 2 * KDIM + VDIM
        EXP = NVH // NKH

        def _l2norm(a):
            n = jnp.sqrt(jnp.sum(a * a, axis=-1, keepdims=True))
            return a / jnp.maximum(n, 1e-12)

        def _reference_tuple_inner(x, W_qkv, W_z, W_b, W_a, conv_w, dt_bias, A_log, norm_w, W_out):
            B, T, _ = x.shape
            qkv = jnp.einsum('bth,ch->btc', x, W_qkv)
            z = jnp.einsum('bth,vh->btv', x, W_z)
            b_raw = jnp.einsum('bth,nh->btn', x, W_b)
            a_raw = jnp.einsum('bth,nh->btn', x, W_a)
            qkv_t = jnp.swapaxes(qkv, 1, 2)
            padded = jnp.concatenate([jnp.zeros((B, CONV, K - 1), x.dtype), qkv_t], axis=2)
            w = conv_w[:, 0, :]
            conv = sum((w[None, :, j:j + 1] * padded[:, :, j:j + T] for j in range(K)))
            conv = jax.nn.silu(conv)
            new_conv_buf = padded[..., T:]
            qkvc = jnp.swapaxes(conv, 1, 2)
            q = qkvc[..., :KDIM].reshape(B, T, NKH, HD)
            kk = qkvc[..., KDIM:2 * KDIM].reshape(B, T, NKH, HD)
            v = qkvc[..., 2 * KDIM:].reshape(B, T, NVH, HD)
            q = jnp.repeat(q, EXP, axis=2)
            kk = jnp.repeat(kk, EXP, axis=2)
            q = _l2norm(q)
            kk = _l2norm(kk)
            beta = jax.nn.sigmoid(b_raw)
            g = -jnp.exp(A_log) * jax.nn.softplus(a_raw + dt_bias)
            decay = jnp.exp(g)
            state0 = jnp.zeros((B, NVH, HD, HD), x.dtype)
            tm = lambda a: jnp.moveaxis(a, 1, 0)

            def step(state, inp):
                q_t, k_t, v_t, b_t, d_t = inp
                state = state * d_t[..., None, None]
                Sk = jnp.einsum('bhi,bhij->bhj', k_t, state)
                delta = (v_t - Sk) * b_t[..., None]
                state = state + jnp.einsum('bhi,bhj->bhij', k_t, delta)
                o = jnp.einsum('bhi,bhij->bhj', q_t, state)
                return (state, o)
            state, o = jax.lax.scan(step, state0, (tm(q), tm(kk), tm(v), tm(beta), tm(decay)))
            o = jnp.moveaxis(o, 0, 1)
            zz = z.reshape(B, T, NVH, HD)
            y = o * jax.nn.silu(zz)
            y = y * jax.lax.rsqrt(jnp.mean(y * y, axis=-1, keepdims=True) + 1e-06) * norm_w
            out = jnp.einsum('btv,ov->bto', y.reshape(B, T, VDIM), W_out)
            return (out, state, new_conv_buf)
        return _reference_tuple_inner(x, W_qkv, W_z, W_b, W_a, conv_w, dt_bias, A_log, norm_w, W_out)[0]

    def _L0_cond2_ref(x, W, A, Bm, scalings, adapter_idx):
        import jax, jax.numpy as jnp
        import numpy as np
        B, T, D_IN, D_OUT = (16, 256, 256, 256)
        N_ADAPTERS, RANK = (8, 16)
        H = jnp.einsum('btd,od->bto', x, W)
        A_b = A[adapter_idx]
        B_b = Bm[adapter_idx]
        s_b = scalings[adapter_idx]
        xa = jnp.einsum('btd,brd->btr', x, A_b)
        delta = jnp.einsum('btr,bor->bto', xa, B_b)
        delta = jax.lax.stop_gradient(delta * s_b[:, None, None])
        return H + delta

    def _L0_ffn_ref(x, W1, W2, W3):
        import jax, jax.numpy as jnp
        import numpy as np
        B, S, D, H = (4, 256, 256, 1024)

        def fwht(x):
            orig_shape = x.shape
            n = orig_shape[-1]
            x = x.reshape(-1, n)
            h = 1
            while h < n:
                xb = x.reshape(-1, n // (2 * h), 2, h)
                a = xb[:, :, 0, :]
                b = xb[:, :, 1, :]
                x = jnp.stack([a + b, a - b], axis=2).reshape(-1, n)
                h *= 2
            scale = jnp.asarray(1.0 / np.sqrt(n), dtype=x.dtype)
            return (x * scale).reshape(orig_shape)
        up_gate = jnp.einsum('bsd,hd->bsh', x, W1)
        up_lin = jnp.einsum('bsd,hd->bsh', x, W3)
        hidden = jax.nn.silu(up_gate) * up_lin
        hidden = fwht(hidden)
        out = jnp.einsum('bsh,dh->bsd', hidden, W2)
        return out
    x = x + _L0_attn_ref(_L0_cond_ref(x, itok_B_1_198, L0_cond_weights), L0_attn_W_qkv, L0_attn_W_z, L0_attn_W_b, L0_attn_W_a, L0_attn_conv_w, L0_attn_dt_bias, L0_attn_A_log, L0_attn_norm_w, L0_attn_W_out)
    x = x + _L0_ffn_ref(_L0_cond2_ref(x, L0_cond2_W, L0_cond2_A, L0_cond2_Bm, L0_cond2_scalings, itok_B_0_6), L0_ffn_W1, L0_ffn_W2, L0_ffn_W3)
    return x

_drawn_inputs = setup_inputs


def setup_inputs(seed=0):
    import zlib

    import numpy as np

    out = dict(_drawn_inputs(seed))
    spreads = {'L0_attn_dt_bias': (1.0, 0.6),
     'L0_attn_A_log': (0.0, 0.674),
     'L0_attn_norm_w': (1.0, 0.2),
     'L0_cond2_scalings': (1.0, 0.6)}
    factors = {'L0_attn_W_a': 2.698}
    for name, (base, spread) in spreads.items():
        noise = np.random.default_rng([zlib.crc32(name.encode()), seed]).standard_normal(out[name].shape)
        drawn = base * np.exp(spread * noise) if base else spread * noise
        out[name] = jnp.asarray(drawn.astype(out[name].dtype))
    for name, factor in factors.items():
        out[name] = (out[name] * factor).astype(out[name].dtype)
    return out
```

```python
from contextlib import ExitStack

import numpy as np

import concourse.bass as bass
from concourse import mybir

F32 = mybir.dt.float32
F32R = mybir.dt.float32r
I32 = mybir.dt.int32
U32 = mybir.dt.uint32
ALU = mybir.AluOpType
ACT = mybir.ActivationFunctionType

P = 128
B, T, HID = 128, 32, 256
NTOK = B * T
QB = P // T
NQUAD = NTOK // P
CH = 512
NCH = NTOK // CH
QC = CH // P
BC = CH // T
KH = HID // P
NKH, NVH, HD, TAPS = 16, 32, 128, 4
NV = NVH // NKH
NSETS = 200
RW = 2 * T + 2
NAD, RANK = 8, 16
FF = 1024
FT = FF // P
NU = NV * NCH


def build_program(nc, x, itok_set, itok_ad, cond_w, w_qk, w_vz, w_o, w_ab, gate_col, norm_w,
                  lora_w, lora_a, lora_b, scal_col, ad_col, w1, w3, w2, had, ident_in, out):
    with ExitStack() as ctx:
        def sb(name, shape, dt=F32):
            return ctx.enter_context(nc.sbuf_tensor(name, shape, dt))

        def sem(name):
            return ctx.enter_context(nc.semaphore(name))

        gathered_d = nc.dram_tensor("gathered_d", [B, T * T], F32, kind="Internal").ap()
        prods_d = nc.dram_tensor("prods_d", [NKH, B, T, RW], F32, kind="Internal").ap()
        mix_d = nc.dram_tensor("mix_d", [NKH, B, NV, T, T], F32, kind="Internal").ap()
        gates_d = nc.dram_tensor("gates_d", [2 * NVH, NTOK], F32, kind="Internal").ap()
        cums_d = nc.dram_tensor("cums_d", [B, NVH, T], F32, kind="Internal").ap()

        xhi = sb("xhi", [P, KH, NTOK], F32R)
        xlo = sb("xlo", [P, KH, NTOK], F32R)
        acc = sb("acc", [P, NQUAD, HID])
        mixbuf = sb("mixbuf", [P, 8192])
        solve = sb("solve", [P, T * RW + 2 * NV * T * T])
        mixT = mixbuf[:, :].rearrange("p (v q t) -> p v q t", v=NV, q=NQUAD)
        prods = solve[:, 0:T * RW].rearrange("p (i c) -> p i c", c=RW)
        E0 = T * RW
        dec = solve[:, E0:E0 + NV * T * T].rearrange("p (v s t) -> p v s t", v=NV, s=T)
        X0 = E0 + NV * T * T
        mix = solve[:, X0:X0 + NV * T * T].rearrange("p (v s t) -> p v s t", v=NV, s=T)
        step_tmp = sb("step_tmp", [P, NV * T * T // 4])
        inv_norm = sb("inv_norm", [P, 2, T])
        gk = sb("gk", [P, 2, NV, T])
        ident = sb("ident", [P, P])
        ones = sb("ones", [P, 8])
        half = sb("half", [P, 2 * T])
        wqk_in = sb("wqk_in", [P, 4 * P + 8])
        wqk_hi = sb("wqk_hi", [P, 4, P], F32R)
        wqk_lo = sb("wqk_lo", [P, 4, P], F32R)
        taps_qk = sb("taps_qk", [P, 2, TAPS])
        wvz_in = sb("wvz_in", [P, 8 * P + 8])
        wvz_hi = sb("wvz_hi", [P, 8, P], F32R)
        wvz_lo = sb("wvz_lo", [P, 8, P], F32R)
        taps_v = sb("taps_v", [P, NV, TAPS])
        wo_in = sb("wo_in", [P, NV * HID])
        wo = sb("wo", [P, NV, HID])
        nw = sb("nw", [P, 1])
        conv = sb("conv", [P, 2, CH])
        qkT = sb("qkT", [P, 2, 2, CH])
        sqq = sb("sqq", [P, CH])
        rows = sb("rows", [P, 2, QC, RW])
        vT = sb("vT", [P, CH])
        vtok = sb("vtok", [P, CH])
        gateT = sb("gateT", [P, CH])
        yT = sb("yT", [P, 2, CH])
        ysq = sb("ysq", [P, CH])
        ms = sb("ms", [P, 2, QC])
        rstd = sb("rstd", [P, 2, QC])
        small = sb("small", [P, 8])
        idx = sb("idx", [P, 2], I32)

        def bank(name, n=1):
            return ctx.enter_context(nc.psum_tensor(name, [P, 512 * n], F32))
        psA, psB, psT, psO, psR, psS = (bank(n) for n in ("psA", "psB", "psT", "psO", "psR", "psS"))
        psW = bank("psW", 2)
        psRv = psR[:, 0:QC * RW].rearrange("p (q c) -> p q c", c=RW)
        psWv = psW[:, :].rearrange("p (q o) -> p q o", o=HID)

        ld_x, ld_idx, ld_gath, st_gath, ld_cw, ld_const, ld_gates = map(sem, (
            "ld_x", "ld_idx", "ld_gath", "st_gath", "ld_cw", "ld_const", "ld_gates"))
        ld_xs = [sem("ld_xs_even"), sem("ld_xs_odd")]
        st_prods = [sem("st_prods_even"), sem("st_prods_odd")]
        zero_cw, cond_mm, cond_hi, cond_lo, gate_mm, gate_ev, wab_split = map(sem, (
            "zero_cw", "cond_mm", "cond_hi", "cond_lo", "gate_mm", "gate_ev", "wab_split"))
        g_act, g_dve, g_sum, st_gates, st_cums, consts_set, zero_mix = map(sem, (
            "g_act", "g_dve", "g_sum", "st_gates", "st_cums", "consts_set", "zero_mix"))
        ld_wqk, ld_wvz, ld_wo, wqk_used, wvz_used, wqk_ready, wvz_ready = map(sem, (
            "ld_wqk", "ld_wvz", "ld_wo", "wqk_used", "wvz_used", "wqk_ready", "wvz_ready"))
        q_mm, k_mm, q_tap, k_tap, q_conv, k_conv, q_ready, k_ready, qk_chain = map(sem, (
            "q_mm", "k_mm", "q_tap", "k_tap", "q_conv", "k_conv", "q_ready", "k_ready", "qk_chain"))
        q_sq, prod_mm, rows_ev, ld_prods = map(sem, ("q_sq", "prod_mm", "rows_ev", "ld_prods"))
        ld_gk, diff_ready, dec_ready, solve_chain, mix_ready, st_mix, ld_mix = map(sem, (
            "ld_gk", "diff_ready", "dec_ready", "solve_chain", "mix_ready", "st_mix", "ld_mix"))
        v_mm, z_mm, v_tap, v_chain, v_conv, v_ready, v_tr, v_tok, z_ready = map(sem, (
            "v_mm", "z_mm", "v_tap", "v_chain", "v_conv", "v_ready", "v_tr", "v_tok", "z_ready"))
        o_mm, y_ready, y_sq, out_mm, ms_ready, rstd_ready, acc_done = map(sem, (
            "o_mm", "y_ready", "y_sq", "out_mm", "ms_ready", "rstd_ready", "acc_done"))
        ld_ffn, had_mm, had_ev, had_add, x1_tr, x1_ev, xa_mm, xa_ev, h_mm, h_ev = map(sem, (
            "ld_ffn", "had_mm", "had_ev", "had_add", "x1_tr", "x1_ev", "xa_mm", "xa_ev", "h_mm", "h_ev"))
        up_mm, lin_mm, up_act, hid_ready, ff_mm, ff_add, st_out, msk = map(sem, (
            "up_mm", "lin_mm", "up_act", "hid_ready", "ff_mm", "ff_add", "st_out", "msk"))

        cw_blk = solve[:, 0:NQUAD * P].rearrange("p (q d) -> p q d", d=P)
        xs = solve[:, 4096:4096 + 2 * QC * HID].rearrange("p (b q h) -> p b q h", b=2, q=QC)
        gath = mixbuf[:, 0:T * T]
        cw = mixbuf[:, 1024:1024 + NQUAD * T].rearrange("p (q d) -> p q d", d=T)
        graw = mixbuf[0:2 * NVH, 4096:4096 + NTOK]
        gtmp = mixbuf[0:2 * NVH, 0:NTOK]
        wab_in = wvz_in[:, 0:KH * P].rearrange("p (k n) -> p k n", n=P)
        gsum = [mixbuf[:, 0:1024].rearrange("p (h t) -> p h t", t=T),
                mixbuf[:, 1024:2048].rearrange("p (h t) -> p h t", t=T)]
        w1s = mixbuf[:, 0:2048].rearrange("p (k n) -> p k n", k=KH)
        w3s = mixbuf[:, 2048:4096].rearrange("p (k n) -> p k n", k=KH)
        w2h = mixbuf[:, 4096:6144].rearrange("p (j o) -> p j o", j=FT)
        lws = mixbuf[:, 6144:6656].rearrange("p (k o) -> p k o", k=KH)
        las = mixbuf[:, 6656:6912].rearrange("p (k o) -> p k o", k=KH)
        lbs = mixbuf[:, 6912:7168]
        x1T = mixbuf[:, 7168:8192].rearrange("p (k n) -> p k n", k=KH)
        hidT = solve[:, 0:4096].rearrange("p (m n) -> p m n", m=FT)
        w2a = solve[:, 0:2048].rearrange("p (j o) -> p j o", j=FT)
        w2b = solve[:, 2048:4096].rearrange("p (j o) -> p j o", j=FT)
        hads = step_tmp[:, 0:P]
        hT = solve[:, 4096:5120].rearrange("p (k n) -> p k n", k=KH)
        xa_m = solve[:, 5120:5632]
        up_s = [vT, vtok]
        maskb = sqq[:, 0:B]
        adi = gateT[:, 0:B].bitcast(I32)
        outs = yT[:, :, :].rearrange("p b n -> p (b n)").rearrange("p (q o) -> p q o", o=HID)

        waits_stood = sem("waits_stood")

        def start_at_one(eng, *sems):
            for s in sems:
                eng.sem_inc(s, 1)

        def alone(eng):
            eng.sem_inc(waits_stood, 1)

        block = ctx.enter_context(nc.Block())

        @block.sync
        def _(sp):
            for s in st_prods:
                sp.sem_inc(s, 16)
            sp.dma_start(idx[:, 0:1], itok_set).then_inc(ld_idx, 16)
            for dst, src in ((ident[:, :], ident_in), (nw[:, :], norm_w),
                             (small[0:2 * NVH, 0:2], gate_col)):
                sp.dma_start(dst, src).then_inc(ld_const, 16)
            sp.dma_start(wab_in, w_ab).then_inc(ld_const, 16)
            sp.dma_start(wqk_in[:, :], w_qk[0]).then_inc(ld_wqk, 16)
            sp.wait_ge(ld_gath, 16)
            sp.dma_start(gathered_d, gath).then_inc(st_gath, 16)
            sp.wait_ge(st_gath, 16)
            sp.dma_start(cw, gathered_d.rearrange("(q b) (c d) -> (b c) q d", b=QB, d=T)).then_inc(ld_cw, 16)
            xq = x.rearrange("(g q b) c h -> g (b c) q h", q=QC, b=QB)
            for p in range(2):
                sp.dma_start(xs[:, p], xq[p]).then_inc(ld_xs[p], 16)
            for g in range(2, NCH):
                sp.wait_ge(cond_mm, g - 1)
                sp.dma_start(xs[:, g % 2], xq[g]).then_inc(ld_xs[g % 2], 16)
            sp.dma_start(acc[:, :, :], x.rearrange("(q b) c h -> (b c) q h", b=QB)).then_inc(ld_x, 16)
            sp.wait_ge(g_dve, 4)
            sp.dma_start(gates_d, graw).then_inc(st_gates, 16)
            sp.wait_ge(st_gates, 16)
            sp.dma_start(gsum[0], gates_d[0:NVH].rearrange("h (b t) -> b h t", t=T)).then_inc(ld_gates, 16)
            sp.wait_ge(g_sum, 5)
            sp.dma_start(cums_d, gsum[1]).then_inc(st_cums, 16)
            sp.wait_ge(st_cums, 16)

            beta_v = gates_d[NVH:2 * NVH].rearrange("(k v) (b t) -> k b v t", v=NV, t=T)
            cums_v = cums_d.rearrange("b (k v) t -> k b v t", v=NV)

            def gate_rows(kk):
                sp.dma_start(gk[:, 0], cums_v[kk]).then_inc(ld_gk, 16)
                sp.dma_start(gk[:, 1], beta_v[kk]).then_inc(ld_gk, 16)

            def products(kk, w0):
                for c in range(NCH):
                    sp.wait_ge(rows_ev, w0 + c + 1 + 1)
                    sp.dma_start(prods_d[kk].rearrange("(c q b) t w -> c (b t) q w", q=QC, b=QB)[c],
                                 rows[:, c % 2]).then_inc(st_prods[c % 2], 16)
                for p in range(2):
                    sp.wait_ge(st_prods[p], (w0 + NCH) * 8 + 16)

            def load_prods(kk):
                sp.dma_start(solve[:, 0:T * RW],
                             prods_d[kk].rearrange("b t w -> b (t w)")).then_inc(ld_prods, 16)

            def store_mix(kk):
                sp.wait_ge(mix_ready, kk + 1)
                sp.dma_start(mix_d[kk].rearrange("b v s t -> b (v s t)"),
                             solve[:, X0:X0 + NV * T * T]).then_inc(st_mix, 16)

            def load_mix(kk):
                sp.wait_ge(st_mix, (kk + 1) * 16)
                src = mix_d[kk].rearrange("(q b) v s t -> b v s q t", b=QB)
                for b in range(QB):
                    for v in range(NV):
                        sp.dma_start(mixT[32 * b:32 * b + 32, v, :, 32 * b:32 * b + 32],
                                     src[b, v]).then_inc(ld_mix, 16)

            gate_rows(0)
            products(0, 0)
            load_prods(0)
            sp.wait_ge(wab_split, 1)
            sp.dma_start(wvz_in[:, :], w_vz[0]).then_inc(ld_wvz, 16)
            sp.dma_start(wo_in[:, :], w_o[0]).then_inc(ld_wo, 16)
            sp.wait_ge(wqk_ready, 1)
            sp.dma_start(wqk_in[:, :], w_qk[1]).then_inc(ld_wqk, 16)
            store_mix(0)
            sp.wait_ge(zero_mix, 1)
            load_mix(0)
            with sp.Fori(0, NKH - 1) as i:
                sp.wait_ge(mix_ready, i + 1)
                gate_rows(i + 1)
                products(i + 1, (i + 1) * NCH)
                load_prods(i + 1)
                sp.wait_ge(wvz_ready, i + 1)
                sp.dma_start(wvz_in[:, :], w_vz[i + 1]).then_inc(ld_wvz, 16)
                sp.dma_start(wo_in[:, :], w_o[i + 1]).then_inc(ld_wo, 16)
                sp.wait_ge(wqk_ready, i + 2)
                sp.dma_start(wqk_in[:, :], w_qk[i + 2]).then_inc(ld_wqk, 16)
                store_mix(i + 1)
                sp.wait_ge(o_mm, (i + 1) * NU + 1)
                alone(sp)
                load_mix(i + 1)
            sp.wait_ge(o_mm, NKH * NU + 1)
            for dst, src in ((w2a, w2), (hads, had), (lws, lora_w), (las, lora_a), (lbs, lora_b),
                             (w1s, w1), (w3s, w3)):
                sp.dma_start(dst, src).then_inc(ld_ffn, 16)
            sp.wait_ge(z_ready, NKH * NU + 1)
            sp.wait_ge(y_ready, NKH * NU + 1)
            sp.dma_start(adi, itok_ad.partition_broadcast(P)).then_inc(ld_ffn, 16)
            sp.dma_start(small[:, 2:3], scal_col).then_inc(ld_ffn, 16)
            sp.dma_start(small[:, 3:4], ad_col).then_inc(ld_ffn, 16)
            outq = out.rearrange("(c q b) t h -> c (b t) q h", q=QC, b=QB)
            with sp.Fori(0, NCH) as c:
                sp.wait_ge(ff_add, c + 1)
                sp.dma_start(outq[c], outs).then_inc(st_out, 16)
            sp.wait_ge(st_out, 16 * NCH)

        @block.gpsimd
        def _(pool):
            pool.wait_ge(ld_idx, 16)
            pool.indirect_dma_start(gath, None, cond_w,
                                    bass.IndirectOffsetOnAxis(ap=idx[:, 0:1].bitcast(U32), axis=0)).then_inc(ld_gath, 16)
            pool.memset(cw_blk, 0.0).then_inc(zero_cw, 1)
            pool.memset(ones[:, :], 1.0)
            pool.memset(half[:, :], -0.5)
            pool.memset(rows[:, :, :, :], 0.0).then_inc(consts_set, 1)

            def split(hi, lo, full, ready, n_hi):
                pool.tensor_copy(hi, full).then_inc(solve_chain, 1)
                pool.wait_ge(solve_chain, n_hi)
                pool.tensor_tensor(lo, full, hi.bitcast(F32), ALU.subtract).then_inc(ready, 1)

            wab_hi = wvz_hi[:, 0:KH, :]
            wab_lo = wvz_lo[:, 0:KH, :]
            pool.wait_ge(ld_const, 16 * 4)
            split(wab_hi, wab_lo, wab_in, wab_split, 1)

            STEPS = T - 1

            def qk_weights(n, ch):
                pool.wait_ge(ld_wqk, (n + 1) * 16)
                alone(pool)
                pool.tensor_copy(taps_qk[:, :, :], wqk_in[:, 4 * P:4 * P + 8].rearrange("p (a b) -> p a b", a=2))
                split(wqk_hi[:, :, :], wqk_lo[:, :, :],
                      wqk_in[:, 0:4 * P].rearrange("p (a b) -> p a b", a=4), wqk_ready, ch + 1)

            def vz_weights(n, ch):
                pool.wait_ge(ld_wvz, (n + 1) * 16)
                pool.wait_ge(ld_wo, (n + 1) * 16)
                alone(pool)
                pool.tensor_copy(taps_v[:, :, :], wvz_in[:, 8 * P:8 * P + 8].rearrange("p (a b) -> p a b", a=2))
                pool.tensor_scalar(wo[:, :, :], wo_in[:, :].rearrange("p (v o) -> p v o", v=NV),
                                   nw[:, 0:1], None, ALU.mult)
                split(wvz_hi[:, :, :], wvz_lo[:, :, :],
                      wvz_in[:, 0:8 * P].rearrange("p (a b) -> p a b", a=8), wvz_ready, ch + 1)

            qk_weights(0, 1)
            pool.wait_ge(ld_gates, 16)
            for n, sh in enumerate((1, 2, 4, 8, 16)):
                a, b = gsum[n % 2], gsum[(n + 1) % 2]
                if n:
                    pool.wait_ge(g_sum, n)
                pool.tensor_copy(b[:, :, 0:sh], a[:, :, 0:sh])
                pool.tensor_tensor(b[:, :, sh:T], a[:, :, sh:T], a[:, :, 0:T - sh], ALU.add).then_inc(g_sum, 1)
            pool.wait_ge(st_cums, 16)
            pool.wait_ge(g_sum, 5)
            pool.memset(mixbuf[:, :], 0.0).then_inc(zero_mix, 1)

            def differences(kk):
                pool.wait_ge(ld_gk, (kk + 1) * 32)
                for v in range(NV):
                    g = gk[:, 0, v, :]
                    pool.tensor_tensor(dec[:, v], g.unsqueeze(1).broadcast_to([P, T, T]),
                                       g.unsqueeze(2).broadcast_to([P, T, T]), ALU.subtract).then_inc(solve_chain, 1)

            def clamp(kk, base):
                pool.wait_ge(solve_chain, base + 2)
                alone(pool)
                pool.tensor_scalar(dec[:, :, :, :], dec[:, :, :, :], 0.0, None, ALU.min).then_inc(diff_ready, 1)

            def solve_parts(kk, base):
                done = [base]

                def link(ins):
                    ins.then_inc(solve_chain, 1)
                    done[0] += 1

                def after():
                    pool.wait_ge(solve_chain, done[0])

                def norms():
                    pool.wait_ge(ld_prods, (kk + 1) * 16)
                    alone(pool)
                    flat = solve[:, 0:T * RW]
                    diag = flat[:, 0:(T - 1) * (RW + 1) + 1:RW + 1]
                    pool.tensor_scalar(inv_norm[:, 0, :], diag, 1e-24, None, ALU.max)
                    link(pool.tensor_scalar(inv_norm[:, 1, :], prods[:, :, 2 * T], 1e-24, None, ALU.max))
                    after()
                    iv = inv_norm[:, :, :].rearrange("p a t -> p (a t)")
                    link(pool.tensor_tensor(iv, iv, half[:, :], ALU.pow))
                    after()
                    link(pool.tensor_tensor(prods[:, :, 0:2 * T], prods[:, :, 0:2 * T],
                                            inv_norm[:, 0, :].unsqueeze(2).broadcast_to([P, T, 2 * T]), ALU.mult))

                def scale():
                    after()
                    row = inv_norm[:, :, :].rearrange("p a t -> p (a t)")
                    link(pool.tensor_tensor(prods[:, :, 0:2 * T], prods[:, :, 0:2 * T],
                                            row.unsqueeze(1).broadcast_to([P, T, 2 * T]), ALU.mult))
                    after()
                    alone(pool)
                    link(pool.affine_select(out=prods[:, :, T:2 * T], in_=prods[:, :, T:2 * T], compare_op=ALU.is_ge,
                                            fill=0.0, base=0, pattern=[[-1, T], [1, T]], channel_multiplier=0))

                def decays():
                    after()
                    pool.wait_ge(dec_ready, kk + 1)
                    if_first_store(kk)
                    link(pool.tensor_tensor(mix[:, :, :, :], dec[:, :, :, :],
                                            prods[:, :, T:2 * T].unsqueeze(1).broadcast_to([P, NV, T, T]), ALU.mult))
                    after()
                    link(pool.tensor_tensor(dec[:, :, :, :], dec[:, :, :, :],
                                            prods[:, :, 0:T].unsqueeze(1).broadcast_to([P, NV, T, T]), ALU.mult))
                    after()
                    link(pool.tensor_tensor(dec[:, :, :, :], dec[:, :, :, :],
                                            gk[:, 1].unsqueeze(2).broadcast_to([P, NV, T, T]), ALU.mult))

                def step(r):
                    n = T - r
                    tmp = step_tmp[:, 0:NV * r * n].rearrange("p (v s t) -> p v s t", v=NV, s=r)
                    after()
                    link(pool.tensor_tensor(tmp, dec[:, :, 0:r, r].unsqueeze(3).broadcast_to([P, NV, r, n]),
                                            mix[:, :, r, r:T].unsqueeze(2).broadcast_to([P, NV, r, n]), ALU.mult))
                    after()
                    link(pool.tensor_tensor(mix[:, :, 0:r, r:T], mix[:, :, 0:r, r:T], tmp, ALU.subtract))

                def last():
                    after()
                    pool.tensor_tensor(mix[:, :, :, :], mix[:, :, :, :],
                                       gk[:, 1].unsqueeze(3).broadcast_to([P, NV, T, T]),
                                       ALU.mult).then_inc(mix_ready, 1)

                def if_first_store(kk_):
                    if not isinstance(kk_, int):
                        pool.wait_ge(st_mix, kk_ * 16)

                return [norms, scale, decays] + [lambda r=r: step(r) for r in range(T - 1, 0, -1)] + [last]

            N_PARTS = 3 + 2 + 3 + 2 * STEPS

            def rstd_of(u, par):
                pool.wait_ge(ms_ready, u + 1)
                pool.tensor_tensor(rstd[:, par, :], ms[:, par, :], half[:, 0:QC], ALU.pow).then_inc(rstd_ready, 1)

            base = 2
            differences(0)
            clamp(0, base)
            for part in solve_parts(0, base + 2):
                part()
            base = base + 2 + N_PARTS
            pool.wait_ge(prod_mm, NCH)
            pool.wait_ge(k_conv, NCH)
            qk_weights(1, base)
            base += 1
            EACH = 1 + 2 + N_PARTS + 1
            with pool.Fori(0, NKH - 1) as i:
                b0 = base + i * EACH
                vz_gate(pool, i, out_mm, v_conv, NU, gate_mm)
                vz_weights(i, b0)
                differences(i + 1)
                clamp(i + 1, b0 + 1)
                parts = solve_parts(i + 1, b0 + 3)
                for j in range(NU):
                    rstd_of(i * NU + j, j % 2)
                    for part in parts[len(parts) * j // NU:len(parts) * (j + 1) // NU]:
                        part()
                pool.wait_ge(prod_mm, (i + 2) * NCH)
                pool.wait_ge(k_conv, (i + 2) * NCH)
                qk_weights(i + 2, b0 + 3 + N_PARTS)
            vz_gate(pool, NKH - 1, out_mm, v_conv, NU, gate_mm)
            vz_weights(NKH - 1, base + (NKH - 1) * EACH)
            for j in range(NU):
                rstd_of((NKH - 1) * NU + j, j % 2)

        @block.tensor
        def _(pe):
            start_at_one(pe, v_tr, o_mm, out_mm)

            def three(ps, hi, lo, k0, cols):
                n = 0
                for k in range(KH):
                    for w, m in ((hi, xhi), (lo, xhi), (hi, xlo)):
                        mm = pe.matmul(ps, w[:, k0 + k, :], m[:, k, cols], start=(n == 0), stop=(n == 3 * KH - 1))
                        n += 1
                return mm

            pe.wait_ge(zero_cw, 2)
            for g in range(NCH):
                pe.wait_ge(ld_xs[g % 2], 16 * (g // 2 + 1))
                if g:
                    pe.wait_ge(cond_hi, g)
                    pe.wait_ge(cond_lo, g)
                for k in range(KH):
                    for q in range(QC):
                        mm = pe.matmul((psA, psB)[k][:, q * P:(q + 1) * P], xs[:, g % 2, q, k * P:(k + 1) * P],
                                       cw_blk[:, g * QC + q, :], start=True, stop=True)
                mm.then_inc(cond_mm, 1)
            pe.wait_ge(wab_split, 1)
            pe.wait_ge(cond_lo, NCH)
            pe.wait_ge(cond_hi, NCH)
            with pe.Fori(0, NCH // 2) as g2:
                for p, ps in ((0, psT), (1, psO)):
                    g = g2 * 2 + p
                    n = 0
                    pe.wait_ge(gate_ev, g2 * 2 + p + 1)
                    three(ps[:, :], wvz_hi, wvz_lo, 0, bass.ds(g2 * (2 * CH) + p * CH, CH)).then_inc(gate_mm, 1)

            def q_proj(w, c):
                pe.wait_ge(q_conv, w + 0) if not isinstance(w, int) or w > 0 else None
                three(psA[:, :], wqk_hi, wqk_lo, 0, bass.ds(c, CH)).then_inc(q_mm, 1)

            def k_proj(w, c):
                pe.wait_ge(k_conv, w + 0) if not isinstance(w, int) or w > 0 else None
                three(psB[:, :], wqk_hi, wqk_lo, KH, bass.ds(c, CH)).then_inc(k_mm, 1)

            def prods_of(w, par, first):
                pe.wait_ge(q_ready, w + 1)
                pe.wait_ge(k_ready, w + 1)
                if not first:
                    pe.wait_ge(rows_ev, w + 1)
                for q in range(QC):
                    for b in range(QB):
                        t0 = q * P + b * T
                        pe.matmul(psRv[b * T:(b + 1) * T, q, 0:2 * T], qkT[:, par, 0, t0:t0 + T],
                                  qkT[:, par, :, t0:t0 + T], start=True, stop=True)
                pe.wait_ge(q_sq, w + 1)
                for q in range(QC):
                    mm = pe.matmul(psRv[:, q, 2 * T:2 * T + 1], sqq[:, q * P:(q + 1) * P], ones[:, 0:1],
                                   start=True, stop=True)
                mm.then_inc(prod_mm, 1)

            def stage1(w0, first):
                if first:
                    q_proj(0, 0)
                    k_proj(0, 0)
                else:
                    q_proj(w0, 0)
                    k_proj(w0, 0)
                with pe.Fori(0, NCH // 2 - 1) as c2:
                    for p in range(2):
                        w = c2 * 2 + (w0 + p)
                        q_proj(w + 1, c2 * (2 * CH) + (p + 1) * CH)
                        k_proj(w + 1, c2 * (2 * CH) + (p + 1) * CH)
                        prods_of(w, p, False)
                q_proj(w0 + (NCH - 1), (NCH - 1) * CH)
                k_proj(w0 + (NCH - 1), (NCH - 1) * CH)
                prods_of(w0 + (NCH - 2), 0, False)
                prods_of(w0 + (NCH - 1), 1, False)

            def v_proj(u, v, c):
                pe.wait_ge(v_conv, u + 1)
                three(psA[:, :], wvz_hi, wvz_lo, 4 * v, bass.ds(c, CH)).then_inc(v_mm, 1)

            def z_proj(u, v, c):
                pe.wait_ge(z_ready, u + 1)
                three(psB[:, :], wvz_hi, wvz_lo, 4 * v + 2, bass.ds(c, CH)).then_inc(z_mm, 1)

            def turn_v(u):
                pe.wait_ge(v_ready, u + 1 + 1)
                pe.wait_ge(v_tok, u + 1)
                for q in range(QC):
                    mm = pe.transpose(psT[:, q * P:(q + 1) * P], vT[:, q * P:(q + 1) * P], ident[:, :])
                mm.then_inc(v_tr, 1)

            def apply_mix(u, v, c):
                pe.wait_ge(v_tok, u + 1 + 1)
                pe.wait_ge(y_ready, u + 1)
                for q in range(QC):
                    mm = pe.matmul(psO[:, q * P:(q + 1) * P], vtok[:, q * P:(q + 1) * P],
                                   mixbuf[:, bass.ds(v * (NQUAD * P) + c + q * P, P)], start=True, stop=True)
                mm.then_inc(o_mm, 1)

            def out_proj(u, v, par):
                pe.wait_ge(y_sq, u + 1)
                pe.wait_ge(acc_done, u + 1)
                for q in range(QC):
                    pe.matmul(psS[:, q:q + 1], ysq[:, q * P:(q + 1) * P], ones[:, 0:1], start=True, stop=True)
                for q in range(QC):
                    mm = pe.matmul(psWv[:, q, :], yT[:, par, q * P:(q + 1) * P], wo[:, v, :], start=True, stop=True)
                mm.then_inc(out_mm, 1)

            def stage2(i):
                u0 = i * NU
                pe.wait_ge(wvz_ready, i + 1)
                pe.wait_ge(ld_mix, (i + 1) * (16 * QB * NV))
                v_proj(u0, 0, 0)

                def slot(u, c, k, head, last):
                    if not last:
                        v_proj(u + 1, (k + 1) % 2, c + (CH if k % 2 else 0))
                    turn_v(u)
                    z_proj(u, k % 2, c)
                    apply_mix(u, k % 2, c)
                    if not head:
                        out_proj(u - 1, (k + 1) % 2, (k + 1) % 2)

                slot(u0, 0, 0, True, False)
                slot(u0 + 1, 0, 1, False, False)
                with pe.Fori(1, NCH - 1) as c:
                    for k in range(2):
                        slot(u0 + c * 2 + k, c * CH, k, False, False)
                slot(u0 + (NU - 2), (NCH - 1) * CH, 0, False, False)
                slot(u0 + (NU - 1), (NCH - 1) * CH, 1, False, True)
                out_proj(u0 + (NU - 1), 1, 1)

            pe.wait_ge(wqk_ready, 1)
            stage1(0, True)
            with pe.Fori(0, NKH - 1) as i:
                pe.wait_ge(wqk_ready, i + 2)
                stage1(i * NCH + NCH, False)
                stage2(i)
            stage2(NKH - 1)

            pe.wait_ge(ld_ffn, 16 * 10)
            for j in range(FT):
                if j >= 2:
                    pe.wait_ge(had_ev, j - 1)
                pe.matmul((psA, psB)[j % 2][:, 0:HID], hads, w2a[:, j, :], start=True, stop=True).then_inc(had_mm, 1)
            pe.wait_ge(had_add, 4)
            for c in range(NCH):
                n0 = c * CH
                pe.wait_ge(acc_done, NKH * NU + 1)
                if c:
                    pe.wait_ge(h_mm, c)
                for k in range(KH):
                    if k or c:
                        pe.wait_ge(x1_ev, KH * c + k)
                    for q in range(QC):
                        mm = pe.transpose(psT[:, q * P:(q + 1) * P], acc[:, c * QC + q, k * P:(k + 1) * P], ident[:, :])
                    mm.then_inc(x1_tr, 1)
                pe.wait_ge(x1_ev, KH * (c + 1))
                if c:
                    pe.wait_ge(xa_ev, c)
                for k in range(KH):
                    mm = pe.matmul(psO[:, :], las[:, k, :], x1T[:, k, :], start=(k == 0), stop=(k == KH - 1))
                mm.then_inc(xa_mm, 1)
                pe.wait_ge(xa_ev, c + 1)
                if c:
                    pe.wait_ge(up_act, FT * c)
                    pe.wait_ge(hid_ready, FT * c)
                for o in range(KH):
                    ps = (psA, psB)[o]
                    for k in range(KH):
                        pe.matmul(ps[:, :], lws[:, k, o * P:(o + 1) * P], x1T[:, k, :], start=(k == 0), stop=False)
                    mm = pe.matmul(ps[:, :], lbs[:, o * P:(o + 1) * P], xa_m, start=False, stop=True)
                mm.then_inc(h_mm, 1)
                pe.wait_ge(h_ev, 2 * (c + 1))
                for m in range(FT):
                    a, bb = ((psA, psB), (psR, psS))[m % 2]
                    n = c * FT + m
                    if m >= 2:
                        pe.wait_ge(hid_ready, n - 1)
                    for ps, w, s in ((a, w1s, up_mm), (bb, w3s, lin_mm)):
                        for k in range(KH):
                            mm = pe.matmul(ps[:, :], w[:, k, m * P:(m + 1) * P], hT[:, k, :], start=(k == 0), stop=(k == KH - 1))
                        mm.then_inc(s, 1)
                pe.wait_ge(hid_ready, FT * (c + 1))
                if c:
                    pe.wait_ge(ff_add, c)
                for q in range(QC):
                    for m in range(FT):
                        mm = pe.matmul(psWv[:, q, :], hidT[:, m, q * P:(q + 1) * P], w2h[:, m, :],
                                       start=(m == 0), stop=(m == FT - 1))
                mm.then_inc(ff_mm, 1)

        @block.scalar
        def _(act):
            start_at_one(act, z_ready, v_tok, v_ready, rows_ev)

            for g in range(NCH):
                act.wait_ge(cond_mm, g + 1)
                act.activation(xhi[:, 0, g * CH:(g + 1) * CH], psA[:, :], ACT.Copy)
                act.activation(xhi[:, 1, g * CH:(g + 1) * CH], psB[:, :], ACT.Copy).then_inc(cond_hi, 1)
            act.sem_inc(gate_ev, 2) if False else None
            act.wait_ge(ld_cw, 16)
            for g in range(NCH):
                if g == 0:
                    act.activation(small[0:1, 6:7], small[0:1, 0:1], ACT.Copy).then_inc(gate_ev, 1)
                act.wait_ge(gate_mm, g + 1) if g else None
                ps = (psT, psO)[g % 2]
                if g == 0:
                    act.activation(small[0:1, 5:6], small[0:1, 0:1], ACT.Copy).then_inc(gate_ev, 1)
                    act.wait_ge(gate_mm, 1)
                act.activation(graw[:, g * CH:(g + 1) * CH], ps[0:2 * NVH, :], ACT.Copy).then_inc(gate_ev, 1)
            a_rows = graw[0:NVH]
            b_rows = graw[NVH:2 * NVH]
            act.wait_ge(gate_ev, NCH + 2)
            act.activation(b_rows, b_rows, ACT.Sigmoid).then_inc(g_act, 1)
            act.activation(small[0:NVH, 4:5], small[0:NVH, 1:2], ACT.Exp).then_inc(g_act, 1)
            act.wait_ge(g_dve, 1)
            act.activation(gtmp[0:NVH], gtmp[0:NVH], ACT.Exp, scale=-1.0).then_inc(g_act, 1)
            act.wait_ge(g_act, 3)
            act.activation(gtmp[0:NVH], gtmp[0:NVH], ACT.Ln, bias=1.0).then_inc(g_act, 1)

            def silu_qk(w, par, first):
                for a, ps, mm, tap in ((0, psA, q_mm, q_tap), (1, psB, k_mm, k_tap)):
                    act.wait_ge(mm, w + 1)
                    if not first:
                        act.wait_ge((q_ready, k_ready)[a], w)
                    act.activation(conv[:, a, :], ps[:, :], ACT.Copy, scale=taps_qk[:, a, TAPS - 1:TAPS]).then_inc(tap, 1)
                for a, cv, rd in ((0, q_conv, q_ready), (1, k_conv, k_ready)):
                    act.wait_ge(cv, w + 1)
                    act.activation(qkT[:, par, 1 - a, :], conv[:, a, :], ACT.Silu).then_inc(rd, 1)
                act.wait_ge(q_ready, w + 1)
                if not first:
                    act.wait_ge(prod_mm, w)
                act.activation(sqq[:, :], qkT[:, par, 1, :], ACT.Square).then_inc(q_sq, 1)

            def rows_out(w, par, first):
                act.wait_ge(prod_mm, w + 1)
                if not first:
                    act.wait_ge(st_prods[par], (w - par) * 8 + 16)
                act.activation(rows[:, par, :, 0:2 * T + 1], psRv[:, :, 0:2 * T + 1], ACT.Copy).then_inc(rows_ev, 1)

            def stage1(w0, first):
                silu_qk(w0, 0, first)
                silu_qk(w0 + 1, 1, False)
                rows_out(w0, 0, first)
                with act.Fori(1, NCH // 2) as c2:
                    for p in range(2):
                        w = c2 * 2 + (w0 + p)
                        silu_qk(w, p, False)
                        rows_out(w - 1, 1 - p, False)
                rows_out(w0 + (NCH - 1), 1, False)

            def tap_v(u, v):
                act.wait_ge(v_mm, u + 1)
                act.wait_ge(v_ready, u + 1)
                act.activation(conv[:, 0, :], psA[:, :], ACT.Copy, scale=taps_v[:, v, TAPS - 1:TAPS]).then_inc(v_tap, 1)

            def silu_v(u):
                act.wait_ge(v_conv, u + 1 + 1)
                act.wait_ge(v_tr, u + 1)
                act.activation(vT[:, :], conv[:, 0, :], ACT.Silu).then_inc(v_ready, 1)

            def stage2(i):
                u0 = i * NU
                act.wait_ge(wvz_ready, i + 1)
                tap_v(u0, 0)
                silu_v(u0)

                def slot(u, k, last):
                    act.wait_ge(v_tr, u + 1 + 1)
                    act.wait_ge(o_mm, u + 1)
                    act.activation(vtok[:, :], psT[:, :], ACT.Copy).then_inc(v_tok, 1)
                    if not last:
                        tap_v(u + 1, 1 - k)
                    act.wait_ge(z_mm, u + 1)
                    act.wait_ge(y_ready, u + 1)
                    act.activation(gateT[:, :], psB[:, :], ACT.Silu).then_inc(z_ready, 1)
                    if not last:
                        silu_v(u + 1)
                    act.wait_ge(y_ready, u + 1 + 1)
                    act.wait_ge(out_mm, u + 1)
                    act.activation(ysq[:, :], yT[:, k, :], ACT.Square).then_inc(y_sq, 1)

                with act.Fori(0, NCH - 1) as c:
                    for k in range(2):
                        slot(u0 + c * 2 + k, k, False)
                slot(u0 + (NU - 2), 0, False)
                slot(u0 + (NU - 1), 1, True)

            def decay_exp(kk):
                act.wait_ge(diff_ready, kk + 1)
                act.activation(dec[:, :, :, :], dec[:, :, :, :], ACT.Exp).then_inc(dec_ready, 1)

            act.wait_ge(wqk_ready, 1)
            act.wait_ge(consts_set, 1)
            stage1(0, True)
            decay_exp(0)
            with act.Fori(0, NKH - 1) as i:
                stage1(i * NCH + NCH, False)
                decay_exp(i + 1)
                stage2(i)
            stage2(NKH - 1)

            for c in range(NCH):
                for o in range(KH):
                    act.wait_ge(h_mm, c + 1)
                    if c:
                        act.wait_ge(lin_mm, FT * c)
                    act.activation(hT[:, o, :], (psA, psB)[o][:, :], ACT.Copy).then_inc(h_ev, 1)
                for m in range(FT):
                    n = c * FT + m
                    act.wait_ge(up_mm, n + 1)
                    if n >= 2:
                        act.wait_ge(hid_ready, n - 1)
                    act.activation(up_s[m % 2][:, :], (psA, psR)[m % 2][:, :], ACT.Silu).then_inc(up_act, 1)

        @block.vector
        def _(dve):
            start_at_one(dve, v_conv, y_ready, acc_done)

            dve.wait_ge(zero_cw, 1)
            dve.wait_ge(ld_cw, 16)
            for b in range(QB):
                last = dve.tensor_copy(cw_blk[32 * b:32 * b + 32, :, 32 * b:32 * b + 32], cw[32 * b:32 * b + 32, :, :])
            last.then_inc(zero_cw, 1)
            for g in range(NCH):
                dve.wait_ge(cond_hi, g + 1)
                for k in range(KH):
                    cols = slice(g * CH, (g + 1) * CH)
                    last = dve.tensor_tensor(xlo[:, k, cols], (psA, psB)[k][:, :], xhi[:, k, cols].bitcast(F32), ALU.subtract)
                last.then_inc(cond_lo, 1)
            a_rows = graw[0:NVH]
            dve.wait_ge(ld_const, 16 * 4)
            dve.wait_ge(gate_ev, NCH + 2)
            dve.tensor_scalar(a_rows, a_rows, small[0:NVH, 0:1], None, ALU.add).then_inc(v_chain, 1)
            dve.wait_ge(v_chain, 1)
            dve.scalar_tensor_tensor(gtmp[0:NVH], a_rows, -1.0, a_rows, ALU.mult, ALU.max).then_inc(g_dve, 1)
            dve.wait_ge(g_act, 4)
            dve.scalar_tensor_tensor(a_rows, a_rows, 0.0, gtmp[0:NVH], ALU.max, ALU.add).then_inc(g_dve, 1)
            dve.wait_ge(g_dve, 2)
            dve.tensor_scalar(a_rows, a_rows, small[0:NVH, 4:5], -1.0, ALU.mult, ALU.mult).then_inc(g_dve, 1)
            dve.wait_ge(g_dve, 3)
            dve.tensor_copy(small[0:1, 6:7], ones[0:1, 0:1]).then_inc(g_dve, 1)

            def tap(dst, ps, w, j):
                d = dst.rearrange("p (b t) -> p b t", t=T)[:, :, j:T]
                s = ps[:, :].rearrange("p (b t) -> p b t", t=T)[:, :, 0:T - j]
                return dve.scalar_tensor_tensor(d, s, w[:, TAPS - 1 - j:TAPS - j], d, ALU.mult, ALU.add)

            def conv_qk(w):
                dve.wait_ge(q_tap, w + 1)
                tap(conv[:, 0, :], psA, taps_qk[:, 0, :], 1).then_inc(qk_chain, 1)
                dve.wait_ge(k_tap, w + 1)
                tap(conv[:, 1, :], psB, taps_qk[:, 1, :], 1).then_inc(qk_chain, 1)
                for n in range(2):
                    for a, ps in ((0, psA), (1, psB)):
                        dve.wait_ge(qk_chain, w * 4 + (2 * n + a + 1 if n == 0 else 3 + a))
                        ins = tap(conv[:, a, :], ps, taps_qk[:, a, :], 2 + n)
                        ins.then_inc(qk_chain if n == 0 else (q_conv, k_conv)[a], 1)

            def stage1(w0):
                with dve.Fori(0, NCH) as c:
                    conv_qk(c + w0)

            def conv_v(u, v):
                dve.wait_ge(v_tap, u + 1)
                for j in (1, 2, 3):
                    if j > 1:
                        dve.wait_ge(v_chain, u * 2 + j)
                    ins = tap(conv[:, 0, :], psA, taps_v[:, v, :], j)
                    ins.then_inc(v_chain if j < 3 else v_conv, 1)

            def gate_y(u, par, head):
                dve.wait_ge(o_mm, u + 1 + 1)
                dve.wait_ge(z_ready, u + 1 + 1)
                if not head:
                    dve.wait_ge(out_mm, u - 1 + 1)
                dve.tensor_tensor(yT[:, par, :], psO[:, :], gateT[:, :], ALU.mult).then_inc(y_ready, 1)

            def add_out(u, par, quad):
                dve.wait_ge(out_mm, u + 1 + 1)
                dve.tensor_scalar(ms[:, par, :], psS[:, 0:QC], 1.0 / HD, 1e-6, ALU.mult, ALU.add).then_inc(ms_ready, 1)
                dve.wait_ge(rstd_ready, u + 1)
                for q in range(QC):
                    a = acc[:, bass.ds(quad + q, 1), :].rearrange("p q o -> p (q o)")
                    last = dve.scalar_tensor_tensor(a, psWv[:, q, :], rstd[:, par, q:q + 1], a, ALU.mult, ALU.add)
                last.then_inc(acc_done, 1)

            def stage2(i):
                u0 = i * NU
                dve.wait_ge(wvz_ready, i + 1)
                conv_v(u0, 0)

                def slot(u, k, quad, head, last):
                    if not last:
                        conv_v(u + 1, 1 - k)
                    gate_y(u, k, head)
                    if not head:
                        add_out(u - 1, 1 - k, quad)

                slot(u0, 0, 0, True, False)
                slot(u0 + 1, 1, 0, False, False)
                with dve.Fori(1, NCH - 1) as c:
                    slot(u0 + c * 2, 0, c * QC - QC, False, False)
                    slot(u0 + c * 2 + 1, 1, c * QC, False, False)
                slot(u0 + (NU - 2), 0, (NCH - 2) * QC, False, False)
                slot(u0 + (NU - 1), 1, (NCH - 1) * QC, False, True)
                add_out(u0 + (NU - 1), 1, (NCH - 1) * QC)

            dve.wait_ge(ld_x, 16)
            dve.wait_ge(wqk_ready, 1)
            stage1(0)
            with dve.Fori(0, NKH - 1) as i:
                dve.wait_ge(wqk_ready, i + 2)
                alone(dve)
                stage1(i * NCH + NCH)
                stage2(i)
            stage2(NKH - 1)

            def lin(j, a):
                return a[:, j, :]
            for j in range(FT):
                dve.wait_ge(had_mm, j + 1)
                dve.tensor_copy(w2b[:, j, :], (psA, psB)[j % 2][:, 0:HID]).then_inc(had_ev, 1)
            src, dst = w2b, w2a
            for n, h in enumerate((1, 2, 4)):
                dve.wait_ge(had_ev, FT)
                if n:
                    dve.wait_ge(had_add, n)
                s = src.rearrange("p (g two r) o -> p g two (r o)", two=2, r=h)
                d = dst.rearrange("p (g two r) o -> p g two (r o)", two=2, r=h)
                dve.tensor_tensor(d[:, :, 0, :], s[:, :, 0, :], s[:, :, 1, :], ALU.add)
                dve.tensor_tensor(d[:, :, 1, :], s[:, :, 0, :], s[:, :, 1, :], ALU.subtract).then_inc(had_add, 1)
                src, dst = dst, src
            dve.wait_ge(had_add, 3)
            dve.tensor_scalar(w2h, src, 1.0 / np.sqrt(FF), None, ALU.mult).then_inc(had_add, 1)
            dve.wait_ge(ld_ffn, 16 * 10)
            dve.wait_ge(q_sq, NKH * NCH)
            dve.tensor_copy(ysq[:, 0:B], adi).then_inc(msk, 1)
            dve.wait_ge(msk, 1)
            dve.tensor_scalar(maskb, ysq[:, 0:B], small[:, 3:4], small[:, 2:3], ALU.is_equal, ALU.mult).then_inc(msk, 1)
            dve.wait_ge(msk, 2)
            for c in range(NCH):
                for k in range(KH):
                    dve.wait_ge(x1_tr, KH * c + k + 1)
                    if c:
                        dve.wait_ge(h_mm, c)
                    dve.tensor_copy(x1T[:, k, :], psT[:, :]).then_inc(x1_ev, 1)
                dve.wait_ge(xa_mm, c + 1)
                dve.tensor_tensor(xa_m.rearrange("p (b t) -> p b t", t=T), psO[:, :].rearrange("p (b t) -> p b t", t=T),
                                  maskb[:, c * BC:(c + 1) * BC].unsqueeze(2).broadcast_to([P, BC, T]),
                                  ALU.mult).then_inc(xa_ev, 1)
                for m in range(FT):
                    n = c * FT + m
                    dve.wait_ge(up_act, n + 1)
                    dve.wait_ge(lin_mm, n + 1)
                    if c:
                        dve.wait_ge(ff_mm, c)
                    dve.tensor_tensor(hidT[:, m, :], (psB, psS)[m % 2][:, :], up_s[m % 2][:, :], ALU.mult).then_inc(hid_ready, 1)
                dve.wait_ge(ff_mm, c + 1)
                if c:
                    dve.wait_ge(st_out, 16 * c)
                dve.tensor_tensor(outs, psWv[:, :, :], acc[:, c * QC:(c + 1) * QC, :], ALU.add).then_inc(ff_add, 1)


def vz_gate(pool, i, out_mm, v_conv, nu, gate_mm):
    if isinstance(i, int) and i == 0:
        return
    pool.wait_ge(gate_mm, NCH)
    pool.wait_ge(out_mm, i * nu + 1)
    pool.wait_ge(v_conv, i * nu + 1)


def kernel(x, itok_B_1_198, itok_B_0_6, L0_cond_weights, L0_attn_W_qkv, L0_attn_W_z, L0_attn_W_b, L0_attn_W_a,
           L0_attn_conv_w, L0_attn_dt_bias, L0_attn_A_log, L0_attn_norm_w, L0_attn_W_out, L0_cond2_W, L0_cond2_A,
           L0_cond2_Bm, L0_cond2_scalings, L0_ffn_W1, L0_ffn_W2, L0_ffn_W3):
    import concourse.bacc as _bacc
    from concourse.bass_utils import run_bass_kernel_spmd as _run

    c = np.ascontiguousarray

    def tiles(w):
        return np.asarray(w).reshape(-1, HD, KH, P).transpose(0, 3, 2, 1)

    wqkv = tiles(L0_attn_W_qkv)
    wz = tiles(L0_attn_W_z)
    taps = np.asarray(L0_attn_conv_w).reshape(-1, HD, TAPS)
    kdim = NKH
    qk = np.concatenate([wqkv[0:kdim].reshape(NKH, P, -1), wqkv[kdim:2 * kdim].reshape(NKH, P, -1),
                         taps[0:kdim], taps[kdim:2 * kdim]], axis=2)
    qk = np.concatenate([qk, qk[:1]], axis=0)
    wv = wqkv[2 * kdim:].reshape(NKH, NV, P, KH * HD)
    wzz = wz.reshape(NKH, NV, P, KH * HD)
    tv = taps[2 * kdim:].reshape(NKH, NV, HD, TAPS)
    vz = np.concatenate([wv[:, 0], wzz[:, 0], wv[:, 1], wzz[:, 1], tv[:, 0], tv[:, 1]], axis=2)
    wo = np.asarray(L0_attn_W_out).T.reshape(NKH, NV, HD, HID).transpose(0, 2, 1, 3).reshape(NKH, HD, NV * HID)
    wab = np.zeros((P, KH, P), np.float32)
    wab[:, :, 0:NVH] = np.asarray(L0_attn_W_a).T.reshape(KH, P, NVH).transpose(1, 0, 2)
    wab[:, :, NVH:2 * NVH] = np.asarray(L0_attn_W_b).T.reshape(KH, P, NVH).transpose(1, 0, 2)
    gcol = np.zeros((2 * NVH, 2), np.float32)
    gcol[0:NVH, 0] = np.asarray(L0_attn_dt_bias)
    gcol[0:NVH, 1] = np.asarray(L0_attn_A_log)
    had = np.ones((1, 1), np.float32)
    while had.shape[0] < P:
        had = np.block([[had, had], [had, -had]])
    rows_of = lambda w, n: np.asarray(w).T.reshape(n, P, -1).transpose(1, 0, 2)
    ins = {
        "x": np.asarray(x),
        "itok_set": np.asarray(itok_B_1_198).reshape(B, 1),
        "itok_ad": np.asarray(itok_B_0_6).reshape(B),
        "cond_w": np.asarray(L0_cond_weights).reshape(NSETS, T * T),
        "w_qk": qk, "w_vz": vz, "w_o": wo, "w_ab": wab, "gate_col": gcol,
        "norm_w": np.asarray(L0_attn_norm_w).reshape(HD, 1),
        "lora_w": rows_of(L0_cond2_W, KH),
        "lora_a": rows_of(np.asarray(L0_cond2_A).reshape(NAD * RANK, HID), KH),
        "lora_b": np.asarray(L0_cond2_Bm).transpose(0, 2, 1).reshape(NAD * RANK, HID),
        "scal_col": np.repeat(np.asarray(L0_cond2_scalings), RANK).reshape(P, 1),
        "ad_col": np.repeat(np.arange(NAD, dtype=np.float32), RANK).reshape(P, 1),
        "w1": rows_of(L0_ffn_W1, KH), "w3": rows_of(L0_ffn_W3, KH), "w2": rows_of(L0_ffn_W2, FT),
        "had": had, "ident_in": np.eye(P, dtype=np.float32),
    }
    nc = _bacc.Bacc("TRN2", target_bir_lowering=False, num_devices=1)
    arrays, args = {}, []
    for name, a in ins.items():
        a = c(a)
        arrays[f"in_{name}"] = a
        args.append(nc.dram_tensor(f"in_{name}", a.shape, mybir.dt.from_np(a.dtype), kind="ExternalInput").ap())
    args.append(nc.dram_tensor("out_0", (B, T, HID), F32, kind="ExternalOutput").ap())
    build_program(nc, *args)
    r = _run(nc, [arrays], core_ids=[0])
    return r.results[0]["out_0"]
```

```python
from contextlib import ExitStack

import numpy as np

import concourse.bass as bass
from concourse import mybir

F32 = mybir.dt.float32
F32R = mybir.dt.float32r
I32 = mybir.dt.int32
U32 = mybir.dt.uint32
ALU = mybir.AluOpType
ACT = mybir.ActivationFunctionType

P = 128
B, T, HID = 128, 32, 256
NTOK = B * T
QB = P // T
NQUAD = NTOK // P
CH = 512
NCH = NTOK // CH
QC = CH // P
BC = CH // T
KH = HID // P
NKH, NVH, HD, TAPS = 16, 32, 128, 4
NV = NVH // NKH
NSETS = 200
RW = 2 * T + 2
NAD, RANK = 8, 16
FF = 1024
FT = FF // P
NU = NV * NCH


def build_program(nc, x, itok_set, itok_ad, cond_w, w_qk, w_vz, w_o, w_ab, gate_col, norm_w,
                  lora_w, lora_a, lora_b, scal_col, ad_col, w1, w3, w2, had, ident_in, out):
    with ExitStack() as ctx:
        def sb(name, shape, dt=F32):
            return ctx.enter_context(nc.sbuf_tensor(name, shape, dt))

        def sem(name):
            return ctx.enter_context(nc.semaphore(name))

        gathered_d = nc.dram_tensor("gathered_d", [B, T * T], F32, kind="Internal").ap()
        prods_d = nc.dram_tensor("prods_d", [NKH, B, T, RW], F32, kind="Internal").ap()
        mix_d = nc.dram_tensor("mix_d", [NKH, B, NV, T, T], F32, kind="Internal").ap()
        gates_d = nc.dram_tensor("gates_d", [2 * NVH, NTOK], F32, kind="Internal").ap()
        cums_d = nc.dram_tensor("cums_d", [B, NVH, T], F32, kind="Internal").ap()

        xhi = sb("xhi", [P, KH, NTOK], F32R)
        xlo = sb("xlo", [P, KH, NTOK], F32R)
        acc = sb("acc", [P, NQUAD, HID])
        mixbuf = sb("mixbuf", [P, 8192])
        solve = sb("solve", [P, T * RW + 2 * NV * T * T])
        mixT = mixbuf[:, :].rearrange("p (v q t) -> p v q t", v=NV, q=NQUAD)
        prods = solve[:, 0:T * RW].rearrange("p (i c) -> p i c", c=RW)
        E0 = T * RW
        dec = solve[:, E0:E0 + NV * T * T].rearrange("p (v s t) -> p v s t", v=NV, s=T)
        X0 = E0 + NV * T * T
        mix = solve[:, X0:X0 + NV * T * T].rearrange("p (v s t) -> p v s t", v=NV, s=T)
        step_tmp = sb("step_tmp", [P, NV * T * T // 4])
        inv_norm = sb("inv_norm", [P, 2, T])
        gk = sb("gk", [P, 2, NV, T])
        ident = sb("ident", [P, P])
        ones = sb("ones", [P, 8])
        half = sb("half", [P, 2 * T])
        wqk_in = sb("wqk_in", [P, 4 * P + 8])
        wqk_hi = sb("wqk_hi", [P, 4, P], F32R)
        wqk_lo = sb("wqk_lo", [P, 4, P], F32R)
        taps_qk = sb("taps_qk", [P, 2, TAPS])
        wvz_in = sb("wvz_in", [P, 8 * P + 8])
        wvz_hi = sb("wvz_hi", [P, 8, P], F32R)
        wvz_lo = sb("wvz_lo", [P, 8, P], F32R)
        taps_v = sb("taps_v", [P, NV, TAPS])
        wo_in = sb("wo_in", [P, NV * HID])
        wo = sb("wo", [P, NV, HID])
        nw = sb("nw", [P, 1])
        conv = sb("conv", [P, 2, CH])
        qkT = sb("qkT", [P, 2, 2, CH])
        sqq = sb("sqq", [P, CH])
        rows = sb("rows", [P, 2, QC, RW])
        vT = sb("vT", [P, CH])
        vtok = sb("vtok", [P, CH])
        gateT = sb("gateT", [P, CH])
        yT = sb("yT", [P, 2, CH])
        ysq = sb("ysq", [P, CH])
        ms = sb("ms", [P, 2, QC])
        rstd = sb("rstd", [P, 2, QC])
        small = sb("small", [P, 8])
        idx = sb("idx", [P, 2], I32)

        def bank(name, n=1):
            return ctx.enter_context(nc.psum_tensor(name, [P, 512 * n], F32))
        psA, psB, psT, psO, psR, psS = (bank(n) for n in ("psA", "psB", "psT", "psO", "psR", "psS"))
        psW = bank("psW", 2)
        psRv = psR[:, 0:QC * RW].rearrange("p (q c) -> p q c", c=RW)
        psWv = psW[:, :].rearrange("p (q o) -> p q o", o=HID)

        qk_banks = ((psA, psB), (psT, psO))
        qk_conv = ((conv[:, 0, :], conv[:, 1, :]), (vtok[:, :], gateT[:, :]))

        ld_x, ld_idx, ld_gath, st_gath, ld_cw, ld_const, ld_gates = map(sem, (
            "ld_x", "ld_idx", "ld_gath", "st_gath", "ld_cw", "ld_const", "ld_gates"))
        ld_xs = [sem("ld_xs_even"), sem("ld_xs_odd")]
        st_prods = [sem("st_prods_even"), sem("st_prods_odd")]
        zero_cw, cond_mm, cond_hi, cond_lo, gate_mm, gate_ev, wab_split = map(sem, (
            "zero_cw", "cond_mm", "cond_hi", "cond_lo", "gate_mm", "gate_ev", "wab_split"))
        g_act, g_dve, g_sum, st_gates, st_cums, consts_set, zero_mix = map(sem, (
            "g_act", "g_dve", "g_sum", "st_gates", "st_cums", "consts_set", "zero_mix"))
        ld_wqk, ld_wvz, ld_wo, wqk_high, wvz_high, wqk_ready, wvz_ready = map(sem, (
            "ld_wqk", "ld_wvz", "ld_wo", "wqk_high", "wvz_high", "wqk_ready", "wvz_ready"))
        q_mm, k_mm, q_tap, k_tap, q_conv, k_conv, q_ready, k_ready, qk_chain = map(sem, (
            "q_mm", "k_mm", "q_tap", "k_tap", "q_conv", "k_conv", "q_ready", "k_ready", "qk_chain"))
        q_sq, prod_mm, rows_ev, ld_prods = map(sem, ("q_sq", "prod_mm", "rows_ev", "ld_prods"))
        ld_cums, ld_betas, diff_ready, diff_chain, dec_ready, solve_chain, mix_ready, st_mix, ld_mix = map(sem, (
            "ld_cums", "ld_betas", "diff_ready", "diff_chain", "dec_ready", "solve_chain", "mix_ready", "st_mix", "ld_mix"))
        v_mm, z_mm, v_tap, v_chain, v_conv, v_ready, v_tr, v_tok, z_ready = map(sem, (
            "v_mm", "z_mm", "v_tap", "v_chain", "v_conv", "v_ready", "v_tr", "v_tok", "z_ready"))
        o_mm, y_ready, y_sq, out_mm, ms_ready, rstd_ready, acc_done = map(sem, (
            "o_mm", "y_ready", "y_sq", "out_mm", "ms_ready", "rstd_ready", "acc_done"))
        ld_ffn, had_mm, had_ev, had_add, x1_tr, x1_ev, xa_mm, xa_ev, h_mm, h_ev = map(sem, (
            "ld_ffn", "had_mm", "had_ev", "had_add", "x1_tr", "x1_ev", "xa_mm", "xa_ev", "h_mm", "h_ev"))
        up_mm, lin_mm, up_act, hid_ready, ff_mm, ff_add, st_out, msk = map(sem, (
            "up_mm", "lin_mm", "up_act", "hid_ready", "ff_mm", "ff_add", "st_out", "msk"))

        cw_blk = solve[:, 0:NQUAD * P].rearrange("p (q d) -> p q d", d=P)
        xs = solve[:, 4096:4096 + 2 * QC * HID].rearrange("p (b q h) -> p b q h", b=2, q=QC)
        gath = mixbuf[:, 0:T * T]
        cw = mixbuf[:, 1024:1024 + NQUAD * T].rearrange("p (q d) -> p q d", d=T)
        graw = mixbuf[0:2 * NVH, 4096:4096 + NTOK]
        gtmp = mixbuf[0:2 * NVH, 0:NTOK]
        wab_in = wvz_in[:, 0:KH * P].rearrange("p (k n) -> p k n", n=P)
        gsum = [mixbuf[:, 0:1024].rearrange("p (h t) -> p h t", t=T),
                mixbuf[:, 1024:2048].rearrange("p (h t) -> p h t", t=T)]
        w1s = mixbuf[:, 0:2048].rearrange("p (k n) -> p k n", k=KH)
        w3s = mixbuf[:, 2048:4096].rearrange("p (k n) -> p k n", k=KH)
        w2h = mixbuf[:, 4096:6144].rearrange("p (j o) -> p j o", j=FT)
        lws = mixbuf[:, 6144:6656].rearrange("p (k o) -> p k o", k=KH)
        las = mixbuf[:, 6656:6912].rearrange("p (k o) -> p k o", k=KH)
        lbs = mixbuf[:, 6912:7168]
        x1T = mixbuf[:, 7168:8192].rearrange("p (k n) -> p k n", k=KH)
        hidT = solve[:, 0:4096].rearrange("p (m n) -> p m n", m=FT)
        w2a = solve[:, 0:2048].rearrange("p (j o) -> p j o", j=FT)
        w2b = solve[:, 2048:4096].rearrange("p (j o) -> p j o", j=FT)
        hads = step_tmp[:, 0:P]
        hT = solve[:, 4096:5120].rearrange("p (k n) -> p k n", k=KH)
        xa_m = solve[:, 5120:5632]
        up_s = [vT, vtok]
        maskb = sqq[:, 0:B]
        adi = gateT[:, 0:B].bitcast(I32)
        outs = yT[:, :, :].rearrange("p b n -> p (b n)").rearrange("p (q o) -> p q o", o=HID)

        waits_stood = sem("waits_stood")

        def start_at_one(eng, *sems):
            for s in sems:
                eng.sem_inc(s, 1)

        def alone(eng):
            eng.sem_inc(waits_stood, 1)

        block = ctx.enter_context(nc.Block())

        @block.sync
        def _(sp):
            sp.dma_start(idx[:, 0:1], itok_set).then_inc(ld_idx, 16)
            for dst, src in ((ident[:, :], ident_in), (nw[:, :], norm_w),
                             (small[0:2 * NVH, 0:2], gate_col)):
                sp.dma_start(dst, src).then_inc(ld_const, 16)
            sp.dma_start(wab_in, w_ab).then_inc(ld_const, 16)
            sp.dma_start(wqk_in[:, :], w_qk[0]).then_inc(ld_wqk, 16)
            sp.wait_ge(ld_gath, 16)
            sp.dma_start(gathered_d, gath).then_inc(st_gath, 16)
            sp.wait_ge(st_gath, 16)
            sp.dma_start(cw, gathered_d.rearrange("(q b) (c d) -> (b c) q d", b=QB, d=T)).then_inc(ld_cw, 16)
            xq = x.rearrange("(g q b) c h -> g (b c) q h", q=QC, b=QB)
            for p in range(2):
                sp.dma_start(xs[:, p], xq[p]).then_inc(ld_xs[p], 16)
            for g in range(2, NCH):
                sp.wait_ge(cond_mm, g - 1)
                sp.dma_start(xs[:, g % 2], xq[g]).then_inc(ld_xs[g % 2], 16)
            sp.dma_start(acc[:, :, :], x.rearrange("(q b) c h -> (b c) q h", b=QB)).then_inc(ld_x, 16)
            sp.wait_ge(g_dve, 4)
            sp.dma_start(gates_d, graw).then_inc(st_gates, 16)
            sp.wait_ge(st_gates, 16)
            sp.dma_start(gsum[0], gates_d[0:NVH].rearrange("h (b t) -> b h t", t=T)).then_inc(ld_gates, 16)
            sp.wait_ge(g_sum, 5)
            sp.dma_start(cums_d, gsum[1]).then_inc(st_cums, 16)
            sp.wait_ge(st_cums, 16)

            beta_v = gates_d[NVH:2 * NVH].rearrange("(k v) (b t) -> k b v t", v=NV, t=T)
            cums_v = cums_d.rearrange("b (k v) t -> k b v t", v=NV)

            def load_decays(kk):
                sp.dma_start(gk[:, 0], cums_v[kk]).then_inc(ld_cums, 16)

            def load_betas(kk):
                sp.dma_start(gk[:, 1], beta_v[kk]).then_inc(ld_betas, 16)

            def products(w0):
                for p in range(2):
                    sp.wait_ge(st_prods[p], (w0 + NCH) * 8 + 16)

            def load_prods(kk):
                sp.dma_start(solve[:, 0:T * RW],
                             prods_d[kk].rearrange("b t w -> b (t w)")).then_inc(ld_prods, 16)

            def store_mix(kk):
                sp.wait_ge(mix_ready, kk + 1)
                sp.dma_start(mix_d[kk].rearrange("b v s t -> b (v s t)"),
                             solve[:, X0:X0 + NV * T * T]).then_inc(st_mix, 16)

            def load_mix(kk):
                sp.wait_ge(st_mix, (kk + 1) * 16)
                src = mix_d[kk].rearrange("(q b) v s t -> b v s q t", b=QB)
                for b in range(QB):
                    for v in range(NV):
                        sp.dma_start(mixT[32 * b:32 * b + 32, v, :, 32 * b:32 * b + 32],
                                     src[b, v]).then_inc(ld_mix, 16)

            load_decays(0)
            load_betas(0)
            products(0)
            load_prods(0)
            sp.wait_ge(wab_split, 1)
            sp.dma_start(wvz_in[:, :], w_vz[0]).then_inc(ld_wvz, 16)
            sp.dma_start(wo_in[:, :], w_o[0]).then_inc(ld_wo, 16)
            sp.wait_ge(wqk_ready, 1)
            sp.dma_start(wqk_in[:, :], w_qk[1]).then_inc(ld_wqk, 16)
            store_mix(0)
            sp.wait_ge(zero_mix, 1)
            load_mix(0)
            with sp.Fori(0, NKH - 1) as i:
                sp.wait_ge(wqk_ready, i + 2)
                sp.dma_start(wqk_in[:, :], w_qk[i + 2]).then_inc(ld_wqk, 16)
                sp.wait_ge(wvz_ready, i + 1)
                sp.dma_start(wvz_in[:, :], w_vz[i + 1]).then_inc(ld_wvz, 16)
                sp.dma_start(wo_in[:, :], w_o[i + 1]).then_inc(ld_wo, 16)
                sp.wait_ge(diff_ready, i + 1)
                load_decays(i + 1)
                products((i + 1) * NCH)
                sp.wait_ge(mix_ready, i + 1)
                load_prods(i + 1)
                load_betas(i + 1)
                store_mix(i + 1)
                sp.wait_ge(o_mm, (i + 1) * NU + 1)
                alone(sp)
                load_mix(i + 1)
            sp.wait_ge(o_mm, NKH * NU + 1)
            for dst, src in ((w2a, w2), (hads, had), (lws, lora_w), (las, lora_a), (lbs, lora_b),
                             (w1s, w1), (w3s, w3)):
                sp.dma_start(dst, src).then_inc(ld_ffn, 16)
            sp.wait_ge(z_ready, NKH * NU + 1)
            sp.wait_ge(y_ready, NKH * NU + 1)
            sp.dma_start(adi, itok_ad.partition_broadcast(P)).then_inc(ld_ffn, 16)
            sp.dma_start(small[:, 2:3], scal_col).then_inc(ld_ffn, 16)
            sp.dma_start(small[:, 3:4], ad_col).then_inc(ld_ffn, 16)
            outq = out.rearrange("(c q b) t h -> c (b t) q h", q=QC, b=QB)
            with sp.Fori(0, NCH) as c:
                sp.wait_ge(ff_add, c + 1)
                sp.dma_start(outq[c], outs).then_inc(st_out, 16)
            sp.wait_ge(st_out, 16 * NCH)

        @block.gpsimd
        def _(pool):
            pool.wait_ge(ld_idx, 16)
            pool.indirect_dma_start(gath, None, cond_w,
                                    bass.IndirectOffsetOnAxis(ap=idx[:, 0:1].bitcast(U32), axis=0)).then_inc(ld_gath, 16)
            pool.memset(cw_blk, 0.0).then_inc(zero_cw, 1)
            pool.memset(ones[:, :], 1.0)
            pool.memset(half[:, :], -0.5)
            pool.memset(rows[:, :, :, :], 0.0).then_inc(consts_set, 1)

            def split(hi, lo, full, ready, n_hi):
                pool.tensor_copy(hi, full).then_inc(solve_chain, 1)
                pool.wait_ge(solve_chain, n_hi)
                pool.tensor_tensor(lo, full, hi.bitcast(F32), ALU.subtract).then_inc(ready, 1)

            wab_hi = wvz_hi[:, 0:KH, :]
            wab_lo = wvz_lo[:, 0:KH, :]
            pool.wait_ge(ld_const, 16 * 4)
            split(wab_hi, wab_lo, wab_in, wab_split, 1)

            STEPS = T - 1
            SLOT_ROOM, FIRST_ROOM = 1800, 1000

            def qk_rest(n):
                pool.wait_ge(wqk_high, n + 1)
                pool.tensor_tensor(wqk_lo[:, :, :], wqk_in[:, 0:4 * P].rearrange("p (a b) -> p a b", a=4),
                                   wqk_hi[:, :, :].bitcast(F32), ALU.subtract).then_inc(wqk_ready, 1)

            def vz_rest(n):
                pool.wait_ge(wvz_high, n + 1)
                pool.tensor_tensor(wvz_lo[:, :, :], wvz_in[:, 0:8 * P].rearrange("p (a b) -> p a b", a=8),
                                   wvz_hi[:, :, :].bitcast(F32), ALU.subtract).then_inc(wvz_ready, 1)

            qk_rest(0)
            pool.wait_ge(ld_gates, 16)
            for n, sh in enumerate((1, 2, 4, 8, 16)):
                a, b = gsum[n % 2], gsum[(n + 1) % 2]
                if n:
                    pool.wait_ge(g_sum, n)
                pool.tensor_copy(b[:, :, 0:sh], a[:, :, 0:sh])
                pool.tensor_tensor(b[:, :, sh:T], a[:, :, sh:T], a[:, :, 0:T - sh], ALU.add).then_inc(g_sum, 1)
            pool.wait_ge(st_cums, 16)
            pool.wait_ge(g_sum, 5)
            pool.memset(mixbuf[:, :], 0.0).then_inc(zero_mix, 1)

            def solve_parts(kk, base):
                done = [base]

                def link(ins):
                    ins.then_inc(solve_chain, 1)
                    done[0] += 1

                def after():
                    pool.wait_ge(solve_chain, done[0])

                def norms():
                    pool.wait_ge(ld_prods, (kk + 1) * 16)
                    alone(pool)
                    flat = solve[:, 0:T * RW]
                    diag = flat[:, 0:(T - 1) * (RW + 1) + 1:RW + 1]
                    pool.tensor_scalar(inv_norm[:, 0, :], diag, 1e-24, None, ALU.max)
                    link(pool.tensor_scalar(inv_norm[:, 1, :], prods[:, :, 2 * T], 1e-24, None, ALU.max))
                    after()
                    iv = inv_norm[:, :, :].rearrange("p a t -> p (a t)")
                    link(pool.tensor_tensor(iv, iv, half[:, :], ALU.pow))
                    after()

                def scale_rows(h):
                    r = slice(h * T // 2, (h + 1) * T // 2)
                    link(pool.tensor_tensor(prods[:, r, 0:2 * T], prods[:, r, 0:2 * T],
                                            inv_norm[:, 0, r].unsqueeze(2).broadcast_to([P, T // 2, 2 * T]), ALU.mult))

                def scale_cols(h):
                    r = slice(h * T // 2, (h + 1) * T // 2)
                    after()
                    row = inv_norm[:, :, :].rearrange("p a t -> p (a t)")
                    link(pool.tensor_tensor(prods[:, r, 0:2 * T], prods[:, r, 0:2 * T],
                                            row.unsqueeze(1).broadcast_to([P, T // 2, 2 * T]), ALU.mult))

                def causal():
                    after()
                    alone(pool)
                    link(pool.affine_select(out=prods[:, :, T:2 * T], in_=prods[:, :, T:2 * T], compare_op=ALU.is_ge,
                                            fill=0.0, base=0, pattern=[[-1, T], [1, T]], channel_multiplier=0))

                def decay_q(v):
                    after()
                    if v == 0:
                        pool.wait_ge(dec_ready, kk + 1)
                        if_first_store(kk)
                    link(pool.tensor_tensor(mix[:, v], dec[:, v], prods[:, :, T:2 * T], ALU.mult))

                def decay_k(v):
                    after()
                    link(pool.tensor_tensor(dec[:, v], dec[:, v], prods[:, :, 0:T], ALU.mult))

                def beta_k(v):
                    if v == 0:
                        pool.wait_ge(ld_betas, (kk + 1) * 16)
                    after()
                    link(pool.tensor_tensor(dec[:, v], dec[:, v],
                                            gk[:, 1, v].unsqueeze(1).broadcast_to([P, T, T]), ALU.mult))

                def step(r):
                    n = T - r
                    tmp = step_tmp[:, 0:NV * r * n].rearrange("p (v s t) -> p v s t", v=NV, s=r)
                    after()
                    link(pool.tensor_tensor(tmp, dec[:, :, 0:r, r].unsqueeze(3).broadcast_to([P, NV, r, n]),
                                            mix[:, :, r, r:T].unsqueeze(2).broadcast_to([P, NV, r, n]), ALU.mult))
                    after()
                    link(pool.tensor_tensor(mix[:, :, 0:r, r:T], mix[:, :, 0:r, r:T], tmp, ALU.subtract))

                def beta_out(v):
                    after()
                    ins = pool.tensor_tensor(mix[:, v], mix[:, v],
                                             gk[:, 1, v].unsqueeze(2).broadcast_to([P, T, T]), ALU.mult)
                    if v == NV - 1:
                        ins.then_inc(mix_ready, 1)
                    else:
                        link(ins)

                def if_first_store(kk_):
                    if not isinstance(kk_, int):
                        pool.wait_ge(st_mix, kk_ * 16)

                half_rows = T * T
                return ([(norms, 400)]
                        + [(lambda h=h: scale_rows(h), half_rows) for h in range(2)]
                        + [(lambda h=h: scale_cols(h), half_rows) for h in range(2)]
                        + [(causal, T * T // 2)]
                        + [(lambda f=f, v=v: f(v), T * T) for f in (decay_q, decay_k, beta_k) for v in range(NV)]
                        + [(lambda r=r: step(r), 2 * NV * r * (T - r) + 80) for r in range(T - 1, 0, -1)]
                        + [(lambda v=v: beta_out(v), T * T) for v in range(NV)])

            N_PARTS = 2 + 2 + 2 + 1 + 3 * NV + 2 * STEPS + (NV - 1)

            def rstd_of(u, par):
                pool.wait_ge(ms_ready, u + 1)
                pool.tensor_tensor(rstd[:, par, :], ms[:, par, :], half[:, 0:QC], ALU.pow).then_inc(rstd_ready, 1)

            for piece, _ in solve_parts(0, 1):
                piece()
            vz_rest(0)
            qk_rest(1)
            with pool.Fori(0, NKH - 1) as i:
                parts = solve_parts(i + 1, i * N_PARTS + (1 + N_PARTS))
                for j in range(NU + 1):
                    if j:
                        rstd_of(i * NU + (j - 1), (j - 1) % 2)
                    if j == 2:
                        qk_rest(i + 2)
                    room = SLOT_ROOM if j else FIRST_ROOM
                    while parts and room >= parts[0][1] // 2:
                        piece, n = parts.pop(0)
                        piece()
                        room -= n
                for piece, _ in parts:
                    piece()
                vz_rest(i + 1)
            for j in range(NU):
                rstd_of((NKH - 1) * NU + j, j % 2)

        @block.tensor
        def _(pe):
            start_at_one(pe, v_tr, o_mm, out_mm)

            def three(ps, hi, lo, k0, cols):
                n = 0
                for k in range(KH):
                    for w, m in ((hi, xhi), (lo, xhi), (hi, xlo)):
                        mm = pe.matmul(ps, w[:, k0 + k, :], m[:, k, cols], start=(n == 0), stop=(n == 3 * KH - 1))
                        n += 1
                return mm

            pe.wait_ge(zero_cw, 2)
            for g in range(NCH):
                pe.wait_ge(ld_xs[g % 2], 16 * (g // 2 + 1))
                if g:
                    pe.wait_ge(cond_hi, g)
                    pe.wait_ge(cond_lo, g)
                for k in range(KH):
                    for q in range(QC):
                        mm = pe.matmul((psA, psB)[k][:, q * P:(q + 1) * P], xs[:, g % 2, q, k * P:(k + 1) * P],
                                       cw_blk[:, g * QC + q, :], start=True, stop=True)
                mm.then_inc(cond_mm, 1)
            pe.wait_ge(wab_split, 1)
            pe.wait_ge(cond_lo, NCH)
            pe.wait_ge(cond_hi, NCH)
            with pe.Fori(0, NCH // 2) as g2:
                for p, ps in ((0, psR), (1, psS)):
                    g = g2 * 2 + p
                    n = 0
                    pe.wait_ge(gate_ev, g2 * 2 + p + 1)
                    three(ps[:, :], wvz_hi, wvz_lo, 0, bass.ds(g2 * (2 * CH) + p * CH, CH)).then_inc(gate_mm, 1)

            def qk_proj(w, par, c, first):
                for a, bank_, conv_done, mm_done in ((0, qk_banks[par][0], q_conv, q_mm),
                                                     (1, qk_banks[par][1], k_conv, k_mm)):
                    if not first:
                        pe.wait_ge(conv_done, w - 1)
                    three(bank_[:, :], wqk_hi, wqk_lo, KH * a, bass.ds(c, CH)).then_inc(mm_done, 1)

            def prods_of(w, par):
                pe.wait_ge(q_ready, w + 1)
                pe.wait_ge(k_ready, w + 1)
                pe.wait_ge(rows_ev, w + 1)
                for q in range(QC):
                    for b in range(QB):
                        t0 = q * P + b * T
                        pe.matmul(psRv[b * T:(b + 1) * T, q, 0:2 * T], qkT[:, par, 0, t0:t0 + T],
                                  qkT[:, par, :, t0:t0 + T], start=True, stop=True)
                pe.wait_ge(q_sq, w + 1)
                for q in range(QC):
                    mm = pe.matmul(psRv[:, q, 2 * T:2 * T + 1], sqq[:, q * P:(q + 1) * P], ones[:, 0:1],
                                   start=True, stop=True)
                mm.then_inc(prod_mm, 1)

            def stage1(w0, first):
                qk_proj(w0, 0, 0, first)
                qk_proj(w0 + 1, 1, CH, first)
                with pe.Fori(0, NCH // 2 - 1) as c2:
                    for p in range(2):
                        w = c2 * 2 + (w0 + p)
                        qk_proj(w + 2, p, c2 * (2 * CH) + (p + 2) * CH, False)
                        prods_of(w, p)
                for p in range(2):
                    prods_of(w0 + (NCH - 2 + p), p)

            def v_proj(u, v, c):
                pe.wait_ge(v_conv, u + 1)
                three(psA[:, :], wvz_hi, wvz_lo, 4 * v, bass.ds(c, CH)).then_inc(v_mm, 1)

            def z_proj(u, v, c):
                pe.wait_ge(z_ready, u + 1)
                three(psB[:, :], wvz_hi, wvz_lo, 4 * v + 2, bass.ds(c, CH)).then_inc(z_mm, 1)

            def turn_v(u):
                pe.wait_ge(v_ready, u + 1 + 1)
                pe.wait_ge(v_tok, u + 1)
                for q in range(QC):
                    mm = pe.transpose(psT[:, q * P:(q + 1) * P], vT[:, q * P:(q + 1) * P], ident[:, :])
                mm.then_inc(v_tr, 1)

            def apply_mix(u, v, c):
                pe.wait_ge(v_tok, u + 1 + 1)
                pe.wait_ge(y_ready, u + 1)
                for q in range(QC):
                    mm = pe.matmul(psO[:, q * P:(q + 1) * P], vtok[:, q * P:(q + 1) * P],
                                   mixbuf[:, bass.ds(v * (NQUAD * P) + c + q * P, P)], start=True, stop=True)
                mm.then_inc(o_mm, 1)

            def out_proj(u, v, par):
                pe.wait_ge(y_sq, u + 1)
                pe.wait_ge(acc_done, u + 1)
                for q in range(QC):
                    pe.matmul(psS[:, q:q + 1], ysq[:, q * P:(q + 1) * P], ones[:, 0:1], start=True, stop=True)
                for q in range(QC):
                    mm = pe.matmul(psWv[:, q, :], yT[:, par, q * P:(q + 1) * P], wo[:, v, :], start=True, stop=True)
                mm.then_inc(out_mm, 1)

            def stage2(i):
                u0 = i * NU
                pe.wait_ge(wvz_ready, i + 1)
                pe.wait_ge(ld_mix, (i + 1) * (16 * QB * NV))
                v_proj(u0, 0, 0)

                def slot(u, c, k, head, last):
                    if not last:
                        v_proj(u + 1, (k + 1) % 2, c + (CH if k % 2 else 0))
                    turn_v(u)
                    z_proj(u, k % 2, c)
                    apply_mix(u, k % 2, c)
                    if not head:
                        out_proj(u - 1, (k + 1) % 2, (k + 1) % 2)

                slot(u0, 0, 0, True, False)
                slot(u0 + 1, 0, 1, False, False)
                with pe.Fori(1, NCH - 1) as c:
                    for k in range(2):
                        slot(u0 + c * 2 + k, c * CH, k, False, False)
                slot(u0 + (NU - 2), (NCH - 1) * CH, 0, False, False)
                slot(u0 + (NU - 1), (NCH - 1) * CH, 1, False, True)
                out_proj(u0 + (NU - 1), 1, 1)

            pe.wait_ge(wqk_ready, 1)
            stage1(0, True)
            with pe.Fori(0, NKH - 1) as i:
                pe.wait_ge(wqk_ready, i + 2)
                stage1(i * NCH + NCH, False)
                stage2(i)
            stage2(NKH - 1)

            pe.wait_ge(ld_ffn, 16 * 10)
            for j in range(FT):
                if j >= 2:
                    pe.wait_ge(had_ev, j - 1)
                pe.matmul((psA, psB)[j % 2][:, 0:HID], hads, w2a[:, j, :], start=True, stop=True).then_inc(had_mm, 1)
            pe.wait_ge(had_add, 4)
            for c in range(NCH):
                n0 = c * CH
                pe.wait_ge(acc_done, NKH * NU + 1)
                if c:
                    pe.wait_ge(h_mm, c)
                for k in range(KH):
                    if k or c:
                        pe.wait_ge(x1_ev, KH * c + k)
                    for q in range(QC):
                        mm = pe.transpose(psT[:, q * P:(q + 1) * P], acc[:, c * QC + q, k * P:(k + 1) * P], ident[:, :])
                    mm.then_inc(x1_tr, 1)
                pe.wait_ge(x1_ev, KH * (c + 1))
                if c:
                    pe.wait_ge(xa_ev, c)
                for k in range(KH):
                    mm = pe.matmul(psO[:, :], las[:, k, :], x1T[:, k, :], start=(k == 0), stop=(k == KH - 1))
                mm.then_inc(xa_mm, 1)
                pe.wait_ge(xa_ev, c + 1)
                if c:
                    pe.wait_ge(up_act, FT * c)
                    pe.wait_ge(hid_ready, FT * c)
                for o in range(KH):
                    ps = (psA, psB)[o]
                    for k in range(KH):
                        pe.matmul(ps[:, :], lws[:, k, o * P:(o + 1) * P], x1T[:, k, :], start=(k == 0), stop=False)
                    mm = pe.matmul(ps[:, :], lbs[:, o * P:(o + 1) * P], xa_m, start=False, stop=True)
                mm.then_inc(h_mm, 1)
                pe.wait_ge(h_ev, 2 * (c + 1))
                for m in range(FT):
                    a, bb = ((psA, psB), (psR, psS))[m % 2]
                    n = c * FT + m
                    if m >= 2:
                        pe.wait_ge(hid_ready, n - 1)
                    for ps, w, s in ((a, w1s, up_mm), (bb, w3s, lin_mm)):
                        for k in range(KH):
                            mm = pe.matmul(ps[:, :], w[:, k, m * P:(m + 1) * P], hT[:, k, :], start=(k == 0), stop=(k == KH - 1))
                        mm.then_inc(s, 1)
                pe.wait_ge(hid_ready, FT * (c + 1))
                if c:
                    pe.wait_ge(ff_add, c)
                for q in range(QC):
                    for m in range(FT):
                        mm = pe.matmul(psWv[:, q, :], hidT[:, m, q * P:(q + 1) * P], w2h[:, m, :],
                                       start=(m == 0), stop=(m == FT - 1))
                mm.then_inc(ff_mm, 1)

        @block.scalar
        def _(act):
            start_at_one(act, z_ready, v_tok, v_ready, rows_ev)
            for s in st_prods:
                act.sem_inc(s, 16)

            for g in range(NCH):
                act.wait_ge(cond_mm, g + 1)
                act.activation(xhi[:, 0, g * CH:(g + 1) * CH], psA[:, :], ACT.Copy)
                act.activation(xhi[:, 1, g * CH:(g + 1) * CH], psB[:, :], ACT.Copy).then_inc(cond_hi, 1)
            act.wait_ge(ld_cw, 16)
            for g in range(NCH):
                if g == 0:
                    act.activation(small[0:1, 6:7], small[0:1, 0:1], ACT.Copy).then_inc(gate_ev, 1)
                act.wait_ge(gate_mm, g + 1) if g else None
                ps = (psR, psS)[g % 2]
                if g == 0:
                    act.activation(small[0:1, 5:6], small[0:1, 0:1], ACT.Copy).then_inc(gate_ev, 1)
                    act.wait_ge(gate_mm, 1)
                act.activation(graw[:, g * CH:(g + 1) * CH], ps[0:2 * NVH, :], ACT.Copy).then_inc(gate_ev, 1)
            a_rows = graw[0:NVH]
            b_rows = graw[NVH:2 * NVH]
            act.wait_ge(gate_ev, NCH + 2)
            act.activation(b_rows, b_rows, ACT.Sigmoid).then_inc(g_act, 1)
            act.activation(small[0:NVH, 4:5], small[0:NVH, 1:2], ACT.Exp).then_inc(g_act, 1)
            act.wait_ge(g_dve, 1)
            act.activation(gtmp[0:NVH], gtmp[0:NVH], ACT.Exp, scale=-1.0).then_inc(g_act, 1)
            act.wait_ge(g_act, 3)
            act.activation(gtmp[0:NVH], gtmp[0:NVH], ACT.Ln, bias=1.0).then_inc(g_act, 1)

            def tap_qk(w, par, first=False):
                for a, mm, tap, rd in ((0, q_mm, q_tap, q_ready), (1, k_mm, k_tap, k_ready)):
                    act.wait_ge(mm, w + 1)
                    if not first:
                        act.wait_ge(rd, w - 1)
                    act.activation(qk_conv[par][a], qk_banks[par][a][:, :], ACT.Copy,
                                   scale=taps_qk[:, a, TAPS - 1:TAPS]).then_inc(tap, 1)

            def silu_qk(w, par, first):
                if not first:
                    act.wait_ge(prod_mm, w - 1)
                for a, cv, rd in ((0, q_conv, q_ready), (1, k_conv, k_ready)):
                    act.wait_ge(cv, w + 1)
                    act.activation(qkT[:, par, 1 - a, :], qk_conv[par][a], ACT.Silu).then_inc(rd, 1)

            def square_q(w, par):
                act.wait_ge(q_ready, w + 1)
                act.activation(sqq[:, :], qkT[:, par, 1, :], ACT.Square).then_inc(q_sq, 1)

            rows_d = prods_d.rearrange("k (c q b) t w -> (k c) (b t) q w", q=QC, b=QB)

            def rows_out(w, par, first):
                act.wait_ge(prod_mm, w + 1)
                if not first:
                    act.wait_ge(st_prods[par], (w - par) * 8 + 16)
                act.activation(rows[:, par, :, 0:2 * T + 1], psRv[:, :, 0:2 * T + 1], ACT.Copy).then_inc(rows_ev, 1)
                act.wait_ge(rows_ev, w + 2)
                act.dma_start(rows_d[w], rows[:, par]).then_inc(st_prods[par], 16)

            def stage1(w0, first):
                tap_qk(w0, 0, first)
                tap_qk(w0 + 1, 1, first)
                silu_qk(w0, 0, first)
                square_q(w0, 0)
                tap_qk(w0 + 2, 0)
                silu_qk(w0 + 1, 1, first)
                rows_out(w0, 0, first)
                square_q(w0 + 1, 1)
                tap_qk(w0 + 3, 1)
                with act.Fori(1, NCH // 2 - 1) as c2:
                    for p in range(2):
                        w = c2 * 2 + (w0 + p)
                        silu_qk(w, p, False)
                        rows_out(w - 1, 1 - p, False)
                        square_q(w, p)
                        tap_qk(w + 2, p)
                for p in range(2):
                    w = w0 + (NCH - 2 + p)
                    silu_qk(w, p, False)
                    rows_out(w - 1, 1 - p, False)
                    square_q(w, p)
                rows_out(w0 + (NCH - 1), 1, False)

            def tap_v(u, v):
                act.wait_ge(v_mm, u + 1)
                act.wait_ge(v_ready, u + 1)
                act.activation(conv[:, 0, :], psA[:, :], ACT.Copy, scale=taps_v[:, v, TAPS - 1:TAPS]).then_inc(v_tap, 1)

            def silu_v(u):
                act.wait_ge(v_conv, u + 1 + 1)
                act.wait_ge(v_tr, u + 1)
                act.activation(vT[:, :], conv[:, 0, :], ACT.Silu).then_inc(v_ready, 1)

            def stage2(i):
                u0 = i * NU
                act.wait_ge(wvz_ready, i + 1)
                tap_v(u0, 0)
                silu_v(u0)

                def slot(u, k, last):
                    act.wait_ge(v_tr, u + 1 + 1)
                    act.wait_ge(o_mm, u + 1)
                    act.activation(vtok[:, :], psT[:, :], ACT.Copy).then_inc(v_tok, 1)
                    if not last:
                        tap_v(u + 1, 1 - k)
                    act.wait_ge(z_mm, u + 1)
                    act.wait_ge(y_ready, u + 1)
                    act.activation(gateT[:, :], psB[:, :], ACT.Silu).then_inc(z_ready, 1)
                    if not last:
                        silu_v(u + 1)
                    act.wait_ge(y_ready, u + 1 + 1)
                    act.wait_ge(out_mm, u + 1)
                    act.activation(ysq[:, :], yT[:, k, :], ACT.Square).then_inc(y_sq, 1)

                with act.Fori(0, NCH - 1) as c:
                    for k in range(2):
                        slot(u0 + c * 2 + k, k, False)
                slot(u0 + (NU - 2), 0, False)
                slot(u0 + (NU - 1), 1, True)

            def qk_high(n):
                act.wait_ge(ld_wqk, (n + 1) * 16)
                act.activation(taps_qk[:, :, :], wqk_in[:, 4 * P:4 * P + 8].rearrange("p (a b) -> p a b", a=2), ACT.Copy)
                act.activation(wqk_hi[:, :, :], wqk_in[:, 0:4 * P].rearrange("p (a b) -> p a b", a=4),
                               ACT.Copy).then_inc(wqk_high, 1)

            def vz_high(n):
                act.wait_ge(ld_wvz, (n + 1) * 16)
                act.wait_ge(ld_wo, (n + 1) * 16)
                act.activation(taps_v[:, :, :], wvz_in[:, 8 * P:8 * P + 8].rearrange("p (a b) -> p a b", a=2), ACT.Copy)
                act.activation(wo[:, :, :], wo_in[:, :].rearrange("p (v o) -> p v o", v=NV), ACT.Copy, scale=nw[:, 0:1])
                act.activation(wvz_hi[:, :, :], wvz_in[:, 0:8 * P].rearrange("p (a b) -> p a b", a=8),
                               ACT.Copy).then_inc(wvz_high, 1)

            def decay_exp(kk):
                act.wait_ge(diff_ready, kk + 1)
                act.activation(dec[:, :, :, :], dec[:, :, :, :], ACT.Exp).then_inc(dec_ready, 1)

            qk_high(0)
            act.wait_ge(consts_set, 1)
            stage1(0, True)
            qk_high(1)
            decay_exp(0)
            act.wait_ge(gate_mm, NCH)
            vz_high(0)
            with act.Fori(0, NKH - 1) as i:
                stage1(i * NCH + NCH, False)
                qk_high(i + 2)
                decay_exp(i + 1)
                stage2(i)
                act.wait_ge(out_mm, i * NU + NU + 1)
                vz_high(i + 1)
            stage2(NKH - 1)

            for c in range(NCH):
                for o in range(KH):
                    act.wait_ge(h_mm, c + 1)
                    if c:
                        act.wait_ge(lin_mm, FT * c)
                    act.activation(hT[:, o, :], (psA, psB)[o][:, :], ACT.Copy).then_inc(h_ev, 1)
                for m in range(FT):
                    n = c * FT + m
                    act.wait_ge(up_mm, n + 1)
                    if n >= 2:
                        act.wait_ge(hid_ready, n - 1)
                    act.activation(up_s[m % 2][:, :], (psA, psR)[m % 2][:, :], ACT.Silu).then_inc(up_act, 1)

        @block.vector
        def _(dve):
            start_at_one(dve, v_conv, y_ready, acc_done)

            dve.wait_ge(zero_cw, 1)
            dve.wait_ge(ld_cw, 16)
            for b in range(QB):
                last = dve.tensor_copy(cw_blk[32 * b:32 * b + 32, :, 32 * b:32 * b + 32], cw[32 * b:32 * b + 32, :, :])
            last.then_inc(zero_cw, 1)
            for g in range(NCH):
                dve.wait_ge(cond_hi, g + 1)
                for k in range(KH):
                    cols = slice(g * CH, (g + 1) * CH)
                    last = dve.tensor_tensor(xlo[:, k, cols], (psA, psB)[k][:, :], xhi[:, k, cols].bitcast(F32), ALU.subtract)
                last.then_inc(cond_lo, 1)
            a_rows = graw[0:NVH]
            dve.wait_ge(ld_const, 16 * 4)
            dve.wait_ge(gate_ev, NCH + 2)
            dve.tensor_scalar(a_rows, a_rows, small[0:NVH, 0:1], None, ALU.add).then_inc(v_chain, 1)
            dve.wait_ge(v_chain, 1)
            dve.scalar_tensor_tensor(gtmp[0:NVH], a_rows, -1.0, a_rows, ALU.mult, ALU.max).then_inc(g_dve, 1)
            dve.wait_ge(g_act, 4)
            dve.scalar_tensor_tensor(a_rows, a_rows, 0.0, gtmp[0:NVH], ALU.max, ALU.add).then_inc(g_dve, 1)
            dve.wait_ge(g_dve, 2)
            dve.tensor_scalar(a_rows, a_rows, small[0:NVH, 4:5], -1.0, ALU.mult, ALU.mult).then_inc(g_dve, 1)
            dve.wait_ge(g_dve, 3)
            dve.tensor_copy(small[0:1, 6:7], ones[0:1, 0:1]).then_inc(g_dve, 1)

            def tap(dst, ps, w, j):
                d = dst.rearrange("p (b t) -> p b t", t=T)[:, :, j:T]
                s = ps[:, :].rearrange("p (b t) -> p b t", t=T)[:, :, 0:T - j]
                return dve.scalar_tensor_tensor(d, s, w[:, TAPS - 1 - j:TAPS - j], d, ALU.mult, ALU.add)

            def differences(kk):
                dve.wait_ge(ld_cums, (kk + 1) * 16)
                if not isinstance(kk, int):
                    dve.wait_ge(mix_ready, kk)
                for v in range(NV):
                    g = gk[:, 0, v, :]
                    last = dve.tensor_tensor(dec[:, v], g.unsqueeze(1).broadcast_to([P, T, T]),
                                             g.unsqueeze(2).broadcast_to([P, T, T]), ALU.subtract)
                last.then_inc(diff_chain, 1)
                dve.wait_ge(diff_chain, kk + 1)
                flat = solve[:, E0:E0 + NV * T * T]
                dve.tensor_scalar(flat, flat, 0.0, None, ALU.min).then_inc(diff_ready, 1)

            def conv_qk(w, par):
                banks, bufs = qk_banks[par], qk_conv[par]
                for n in range(3):
                    for a in range(2):
                        if n == 0:
                            dve.wait_ge((q_tap, k_tap)[a], w + 1)
                        else:
                            dve.wait_ge(qk_chain, w * 4 + (2 * n - 1 + a))
                        tap(bufs[a], banks[a], taps_qk[:, a, :], n + 1).then_inc(
                            qk_chain if n < 2 else (q_conv, k_conv)[a], 1)

            def stage1(w0):
                with dve.Fori(0, NCH // 2) as c2:
                    for p in range(2):
                        conv_qk(c2 * 2 + (w0 + p), p)

            def conv_v(u, v):
                dve.wait_ge(v_tap, u + 1)
                for j in (1, 2, 3):
                    if j > 1:
                        dve.wait_ge(v_chain, u * 2 + j)
                    ins = tap(conv[:, 0, :], psA, taps_v[:, v, :], j)
                    ins.then_inc(v_chain if j < 3 else v_conv, 1)

            def gate_y(u, par, head):
                dve.wait_ge(o_mm, u + 1 + 1)
                dve.wait_ge(z_ready, u + 1 + 1)
                if not head:
                    dve.wait_ge(out_mm, u - 1 + 1)
                dve.tensor_tensor(yT[:, par, :], psO[:, :], gateT[:, :], ALU.mult).then_inc(y_ready, 1)

            def add_out(u, par, quad):
                dve.wait_ge(out_mm, u + 1 + 1)
                dve.tensor_scalar(ms[:, par, :], psS[:, 0:QC], 1.0 / HD, 1e-6, ALU.mult, ALU.add).then_inc(ms_ready, 1)
                dve.wait_ge(rstd_ready, u + 1)
                for q in range(QC):
                    a = acc[:, bass.ds(quad + q, 1), :].rearrange("p q o -> p (q o)")
                    last = dve.scalar_tensor_tensor(a, psWv[:, q, :], rstd[:, par, q:q + 1], a, ALU.mult, ALU.add)
                last.then_inc(acc_done, 1)

            def stage2(i):
                u0 = i * NU
                dve.wait_ge(wvz_ready, i + 1)
                conv_v(u0, 0)

                def slot(u, k, quad, head, last):
                    if not last:
                        conv_v(u + 1, 1 - k)
                    gate_y(u, k, head)
                    if not head:
                        add_out(u - 1, 1 - k, quad)

                slot(u0, 0, 0, True, False)
                slot(u0 + 1, 1, 0, False, False)
                with dve.Fori(1, NCH - 1) as c:
                    slot(u0 + c * 2, 0, c * QC - QC, False, False)
                    slot(u0 + c * 2 + 1, 1, c * QC, False, False)
                slot(u0 + (NU - 2), 0, (NCH - 2) * QC, False, False)
                slot(u0 + (NU - 1), 1, (NCH - 1) * QC, False, True)
                add_out(u0 + (NU - 1), 1, (NCH - 1) * QC)

            dve.wait_ge(ld_x, 16)
            dve.wait_ge(wqk_ready, 1)
            stage1(0)
            differences(0)
            with dve.Fori(0, NKH - 1) as i:
                dve.wait_ge(wqk_ready, i + 2)
                alone(dve)
                stage1(i * NCH + NCH)
                differences(i + 1)
                stage2(i)
            stage2(NKH - 1)

            for j in range(FT):
                dve.wait_ge(had_mm, j + 1)
                dve.tensor_copy(w2b[:, j, :], (psA, psB)[j % 2][:, 0:HID]).then_inc(had_ev, 1)
            src, dst = w2b, w2a
            for n, h in enumerate((1, 2, 4)):
                dve.wait_ge(had_ev, FT)
                if n:
                    dve.wait_ge(had_add, n)
                s = src.rearrange("p (g two r) o -> p g two (r o)", two=2, r=h)
                d = dst.rearrange("p (g two r) o -> p g two (r o)", two=2, r=h)
                dve.tensor_tensor(d[:, :, 0, :], s[:, :, 0, :], s[:, :, 1, :], ALU.add)
                dve.tensor_tensor(d[:, :, 1, :], s[:, :, 0, :], s[:, :, 1, :], ALU.subtract).then_inc(had_add, 1)
                src, dst = dst, src
            dve.wait_ge(had_add, 3)
            dve.tensor_scalar(w2h, src, 1.0 / np.sqrt(FF), None, ALU.mult).then_inc(had_add, 1)
            dve.wait_ge(ld_ffn, 16 * 10)
            dve.wait_ge(q_sq, NKH * NCH)
            dve.tensor_copy(ysq[:, 0:B], adi).then_inc(msk, 1)
            dve.wait_ge(msk, 1)
            dve.tensor_scalar(maskb, ysq[:, 0:B], small[:, 3:4], small[:, 2:3], ALU.is_equal, ALU.mult).then_inc(msk, 1)
            dve.wait_ge(msk, 2)
            for c in range(NCH):
                for k in range(KH):
                    dve.wait_ge(x1_tr, KH * c + k + 1)
                    if c:
                        dve.wait_ge(h_mm, c)
                    dve.tensor_copy(x1T[:, k, :], psT[:, :]).then_inc(x1_ev, 1)
                dve.wait_ge(xa_mm, c + 1)
                dve.tensor_tensor(xa_m.rearrange("p (b t) -> p b t", t=T), psO[:, :].rearrange("p (b t) -> p b t", t=T),
                                  maskb[:, c * BC:(c + 1) * BC].unsqueeze(2).broadcast_to([P, BC, T]),
                                  ALU.mult).then_inc(xa_ev, 1)
                for m in range(FT):
                    n = c * FT + m
                    dve.wait_ge(up_act, n + 1)
                    dve.wait_ge(lin_mm, n + 1)
                    if c:
                        dve.wait_ge(ff_mm, c)
                    dve.tensor_tensor(hidT[:, m, :], (psB, psS)[m % 2][:, :], up_s[m % 2][:, :], ALU.mult).then_inc(hid_ready, 1)
                dve.wait_ge(ff_mm, c + 1)
                if c:
                    dve.wait_ge(st_out, 16 * c)
                dve.tensor_tensor(outs, psWv[:, :, :], acc[:, c * QC:(c + 1) * QC, :], ALU.add).then_inc(ff_add, 1)


def kernel(x, itok_B_1_198, itok_B_0_6, L0_cond_weights, L0_attn_W_qkv, L0_attn_W_z, L0_attn_W_b, L0_attn_W_a,
           L0_attn_conv_w, L0_attn_dt_bias, L0_attn_A_log, L0_attn_norm_w, L0_attn_W_out, L0_cond2_W, L0_cond2_A,
           L0_cond2_Bm, L0_cond2_scalings, L0_ffn_W1, L0_ffn_W2, L0_ffn_W3):
    import concourse.bacc as _bacc
    from concourse.bass_utils import run_bass_kernel_spmd as _run

    c = np.ascontiguousarray

    def tiles(w):
        return np.asarray(w).reshape(-1, HD, KH, P).transpose(0, 3, 2, 1)

    wqkv = tiles(L0_attn_W_qkv)
    wz = tiles(L0_attn_W_z)
    taps = np.asarray(L0_attn_conv_w).reshape(-1, HD, TAPS)
    kdim = NKH
    qk = np.concatenate([wqkv[0:kdim].reshape(NKH, P, -1), wqkv[kdim:2 * kdim].reshape(NKH, P, -1),
                         taps[0:kdim], taps[kdim:2 * kdim]], axis=2)
    qk = np.concatenate([qk, qk[:1]], axis=0)
    wv = wqkv[2 * kdim:].reshape(NKH, NV, P, KH * HD)
    wzz = wz.reshape(NKH, NV, P, KH * HD)
    tv = taps[2 * kdim:].reshape(NKH, NV, HD, TAPS)
    vz = np.concatenate([wv[:, 0], wzz[:, 0], wv[:, 1], wzz[:, 1], tv[:, 0], tv[:, 1]], axis=2)
    wo = np.asarray(L0_attn_W_out).T.reshape(NKH, NV, HD, HID).transpose(0, 2, 1, 3).reshape(NKH, HD, NV * HID)
    wab = np.zeros((P, KH, P), np.float32)
    wab[:, :, 0:NVH] = np.asarray(L0_attn_W_a).T.reshape(KH, P, NVH).transpose(1, 0, 2)
    wab[:, :, NVH:2 * NVH] = np.asarray(L0_attn_W_b).T.reshape(KH, P, NVH).transpose(1, 0, 2)
    gcol = np.zeros((2 * NVH, 2), np.float32)
    gcol[0:NVH, 0] = np.asarray(L0_attn_dt_bias)
    gcol[0:NVH, 1] = np.asarray(L0_attn_A_log)
    had = np.ones((1, 1), np.float32)
    while had.shape[0] < P:
        had = np.block([[had, had], [had, -had]])
    rows_of = lambda w, n: np.asarray(w).T.reshape(n, P, -1).transpose(1, 0, 2)
    ins = {
        "x": np.asarray(x),
        "itok_set": np.asarray(itok_B_1_198).reshape(B, 1),
        "itok_ad": np.asarray(itok_B_0_6).reshape(B),
        "cond_w": np.asarray(L0_cond_weights).reshape(NSETS, T * T),
        "w_qk": qk, "w_vz": vz, "w_o": wo, "w_ab": wab, "gate_col": gcol,
        "norm_w": np.asarray(L0_attn_norm_w).reshape(HD, 1),
        "lora_w": rows_of(L0_cond2_W, KH),
        "lora_a": rows_of(np.asarray(L0_cond2_A).reshape(NAD * RANK, HID), KH),
        "lora_b": np.asarray(L0_cond2_Bm).transpose(0, 2, 1).reshape(NAD * RANK, HID),
        "scal_col": np.repeat(np.asarray(L0_cond2_scalings), RANK).reshape(P, 1),
        "ad_col": np.repeat(np.arange(NAD, dtype=np.float32), RANK).reshape(P, 1),
        "w1": rows_of(L0_ffn_W1, KH), "w3": rows_of(L0_ffn_W3, KH), "w2": rows_of(L0_ffn_W2, FT),
        "had": had, "ident_in": np.eye(P, dtype=np.float32),
    }
    nc = _bacc.Bacc("TRN2", target_bir_lowering=False, num_devices=1)
    arrays, args = {}, []
    for name, a in ins.items():
        a = c(a)
        arrays[f"in_{name}"] = a
        args.append(nc.dram_tensor(f"in_{name}", a.shape, mybir.dt.from_np(a.dtype), kind="ExternalInput").ap())
    args.append(nc.dram_tensor("out_0", (B, T, HID), F32, kind="ExternalOutput").ap())
    build_program(nc, *args)
    r = _run(nc, [arrays], core_ids=[0])
    return r.results[0]["out_0"]
```

```python
from contextlib import ExitStack

import numpy as np

import concourse.bass as bass
from concourse import mybir

F32 = mybir.dt.float32
F32R = mybir.dt.float32r
I32 = mybir.dt.int32
U32 = mybir.dt.uint32
ALU = mybir.AluOpType
ACT = mybir.ActivationFunctionType

P = 128
B, T, HID = 128, 32, 256
NTOK = B * T
QB = P // T
NQUAD = NTOK // P
CH = 512
NCH = NTOK // CH
QC = CH // P
BC = CH // T
KH = HID // P
NKH, NVH, HD, TAPS = 16, 32, 128, 4
NV = NVH // NKH
NSETS = 200
RW = 2 * T + 1
NAD, RANK = 8, 16
FF = 1024
FT = FF // P
NU = NV * NCH


def build_program(nc, x, itok_set, itok_ad, cond_w, w_qk, w_vz, w_o, w_ab, gate_col, norm_w,
                  lora_w, lora_a, lora_b, scal_col, ad_col, w1, w3, w2, had, ident_in, out):
    with ExitStack() as ctx:
        def sb(name, shape, dt=F32):
            return ctx.enter_context(nc.sbuf_tensor(name, shape, dt))

        def sem(name):
            return ctx.enter_context(nc.semaphore(name))

        gathered_d = nc.dram_tensor("gathered_d", [B, T * T], F32, kind="Internal").ap()
        prods_d = nc.dram_tensor("prods_d", [NKH, B, T, RW], F32, kind="Internal").ap()
        mix_d = nc.dram_tensor("mix_d", [NKH, B, NV, T, T], F32, kind="Internal").ap()
        gates_d = nc.dram_tensor("gates_d", [2 * NVH, NTOK], F32, kind="Internal").ap()
        cums_d = nc.dram_tensor("cums_d", [B, NVH, T], F32, kind="Internal").ap()

        xhi = sb("xhi", [P, KH, NTOK], F32R)
        xlo = sb("xlo", [P, KH, NTOK], F32R)
        acc = sb("acc", [P, NQUAD, HID])
        mixbuf = sb("mixbuf", [P, 8192], F32R)
        solve = sb("solve", [P, T * RW + 2 * NV * T * T])
        mixf = mixbuf[:, :].bitcast(F32)
        mixT = mixf.rearrange("p (v q t) -> p v q t", v=NV, q=NQUAD)
        prods = solve[:, 0:T * RW].rearrange("p (i c) -> p i c", c=RW)
        E0 = T * RW
        dec = solve[:, E0:E0 + NV * T * T].rearrange("p (v s t) -> p v s t", v=NV, s=T)
        X0 = E0 + NV * T * T
        mix = solve[:, X0:X0 + NV * T * T].rearrange("p (v s t) -> p v s t", v=NV, s=T)
        step_tmp = sb("step_tmp", [P, NV * T * T // 4])
        inv_norm = sb("inv_norm", [P, 2, T])
        gk = sb("gk", [P, 2, NV, T])
        ident = sb("ident", [P, P])
        ones = sb("ones", [P, 1])
        half = sb("half", [P, T // 4])
        wqk_in = sb("wqk_in", [P, 4 * P + 8])
        wqk_hi = sb("wqk_hi", [P, 4, P], F32R)
        wqk_lo = sb("wqk_lo", [P, 4, P], F32R)
        taps_qk = sb("taps_qk", [P, 2, TAPS])
        wvz_in = sb("wvz_in", [P, 8 * P + 8])
        wvz_hi = sb("wvz_hi", [P, 8, P], F32R)
        wvz_lo = sb("wvz_lo", [P, 8, P], F32R)
        taps_v = sb("taps_v", [P, NV, TAPS])
        wo_in = sb("wo_in", [P, NV * HID])
        wo_hi = sb("wo_hi", [P, NV, HID], F32R)
        wo_lo = sb("wo_lo", [P, NV, HID], F32R)
        nw = sb("nw", [P, 1])
        conv = sb("conv", [P, 2, CH])
        qkT = sb("qkT", [P, 2, 2, CH])
        y_halves = sb("y_halves", [P, 2, 2, CH], F32R)
        y_hi, y_lo = ([y_halves[:, h, p, :] for p in range(2)] for h in range(2))
        sqq = sb("sqq", [P, CH])
        rows = sb("rows", [P, 2, QC, RW])
        vT = qkT[:, 0, 0, :]
        vtok = sb("vtok", [P, CH])
        gateT = sb("gateT", [P, CH])
        yT = qkT[:, 0, 1, :]
        ysq = sqq
        ms = sb("ms", [P, 2, QC])
        rstd = sb("rstd", [P, 2, QC])
        small = sb("small", [P, 8])
        idx = sb("idx", [P, 2], I32)

        def bank(name, n=1):
            return ctx.enter_context(nc.psum_tensor(name, [P, 512 * n], F32))
        psA, psB, psT, psO, psR, psS = (bank(n) for n in ("psA", "psB", "psT", "psO", "psR", "psS"))
        psW = bank("psW", 2)
        psRv = psR[:, 0:QC * RW].rearrange("p (q c) -> p q c", c=RW)
        psWv = psW[:, :].rearrange("p (q o) -> p q o", o=HID)

        qk_banks = ((psA, psB), (psT, psO))
        qk_conv = ((conv[:, 0, :], conv[:, 1, :]), (vtok[:, :], gateT[:, :]))

        ld_x, ld_idx, ld_gath, st_gath, ld_cw, ld_const, ld_gates = map(sem, (
            "ld_x", "ld_idx", "ld_gath", "st_gath", "ld_cw", "ld_const", "ld_gates"))
        ld_xs = [sem("ld_xs_even"), sem("ld_xs_odd")]
        st_prods = [sem("st_prods_even"), sem("st_prods_odd")]
        zero_cw, cond_mm, cond_hi, cond_lo, gate_mm, gate_ev, wab_split = map(sem, (
            "zero_cw", "cond_mm", "cond_hi", "cond_lo", "gate_mm", "gate_ev", "wab_split"))
        betas_act, st_betas, dve_steps = map(sem, ("betas_act", "st_betas", "dve_steps"))
        g_act, g_dve, g_sum, st_gates, st_cums, consts_set, zero_mix = map(sem, (
            "g_act", "g_dve", "g_sum", "st_gates", "st_cums", "consts_set", "zero_mix"))
        ld_wqk, ld_wvz, ld_wo, wqk_high, wvz_high, wqk_ready, wvz_ready = map(sem, (
            "ld_wqk", "ld_wvz", "ld_wo", "wqk_high", "wvz_high", "wqk_ready", "wvz_ready"))
        q_mm, k_mm, q_tap, k_tap, q_conv, k_conv, q_ready, k_ready, qk_chain = map(sem, (
            "q_mm", "k_mm", "q_tap", "k_tap", "q_conv", "k_conv", "q_ready", "k_ready", "qk_chain"))
        q_sq, prod_mm, rows_ev, ld_prods = map(sem, ("q_sq", "prod_mm", "rows_ev", "ld_prods"))
        ld_cums, ld_betas, diff_ready, diff_chain, dec_ready, solve_chain, mix_ready, st_mix, ld_mix = map(sem, (
            "ld_cums", "ld_betas", "diff_ready", "diff_chain", "dec_ready", "solve_chain", "mix_ready", "st_mix", "ld_mix"))
        v_mm, z_mm, v_tap, v_chain, v_conv, v_ready, v_tr, v_tok, z_ready = map(sem, (
            "v_mm", "z_mm", "v_tap", "v_chain", "v_conv", "v_ready", "v_tr", "v_tok", "z_ready"))
        y_high, y_low, wo_ready = map(sem, ("y_high", "y_low", "wo_ready"))
        o_mm, y_ready, y_sq, out_mm, ms_ready, rstd_ready, acc_done = map(sem, (
            "o_mm", "y_ready", "y_sq", "out_mm", "ms_ready", "rstd_ready", "acc_done"))
        ld_ffn, had_mm, had_ev, had_add, w2_ready, w_high, w_low, lora_high, lora_low, msk = map(sem, (
            "ld_ffn", "had_mm", "had_ev", "had_add", "w2_ready", "w_high", "w_low", "lora_high",
            "lora_low", "msk"))
        x1_copy, x1_tr, x1_high, x1_low, xa_mm, xa_f, xa_high, xa_low, h_mm, h_high, h_low = map(sem, (
            "x1_copy", "x1_tr", "x1_high", "x1_low", "xa_mm", "xa_f", "xa_high", "xa_low", "h_mm", "h_high", "h_low"))
        up_mm, lin_mm, up_act, hid_f, hid_high, hid_low, ff_mm, ff_add, st_out = map(sem, (
            "up_mm", "lin_mm", "up_act", "hid_f", "hid_high", "hid_low", "ff_mm", "ff_add", "st_out"))

        cw_blk = solve[:, 0:NQUAD * P].rearrange("p (q d) -> p q d", d=P)
        xs = solve[:, 4096:4096 + 2 * QC * HID].rearrange("p (b q h) -> p b q h", b=2, q=QC)
        early = acc[:, :, :].rearrange("p q h -> p (q h)")
        gath = early[:, 0:T * T]
        cw = early[:, 1024:1024 + NQUAD * T].rearrange("p (q d) -> p q d", d=T)
        graw = early[0:2 * NVH, 4096:4096 + NTOK]
        gtmp = early[0:2 * NVH, 0:NTOK]
        wab_in = wvz_in[:, 0:KH * P].rearrange("p (k n) -> p k n", n=P)
        gsum = [early[:, 0:1024].rearrange("p (h t) -> p h t", t=T),
                early[:, 1024:2048].rearrange("p (h t) -> p h t", t=T)]
        w1_in = solve[:, 0:2048].rearrange("p (k n) -> p k n", k=KH)
        w3_in = solve[:, 2048:4096].rearrange("p (k n) -> p k n", k=KH)
        w2_in = solve[:, 4096:6144].rearrange("p (j o) -> p j o", j=FT)
        lw_in = wqk_in[:, 0:KH * HID].rearrange("p (k o) -> p k o", k=KH)
        la_in = step_tmp[:, 0:HID].rearrange("p (k o) -> p k o", k=KH)
        lb_in = step_tmp[:, HID:2 * HID]
        hads = wo_in[:, 0:P]
        halves = [xh[:, :, :].rearrange("p k n -> p (k n)") for xh in (xhi, xlo)]
        w1h, w2h, w3h, lah, lbh, x1h, xah = ([h[:, a:b] for h in halves] for a, b in (
            (0, 2048), (2048, 4096), (4096, 6144), (6144, 6400), (6400, 6656), (6656, 7680), (7680, 8192)))
        lwh = [w[:, :, :].rearrange("p a b -> p (a b)") for w in (wqk_hi, wqk_lo)]
        w1h, w3h, lwh, lah, x1h = ([h.rearrange("p (k n) -> p k n", k=KH) for h in hs] for hs in (w1h, w3h, lwh, lah, x1h))
        w2h = [h.rearrange("p (j o) -> p j o", j=FT) for h in w2h]
        hidh = [mixbuf[:, n * 4096:(n + 1) * 4096].rearrange("p (m n) -> p m n", m=FT) for n in range(2)]
        hTh = [w[:, :, :].rearrange("p a b -> p (a b)").rearrange("p (k n) -> p k n", k=KH) for w in (wvz_hi, wvz_lo)]
        w2a = solve[:, 0:2048].rearrange("p (j o) -> p j o", j=FT)
        w2b = solve[:, 2048:4096].rearrange("p (j o) -> p j o", j=FT)
        x1c = wvz_in[:, 0:QC * HID].rearrange("p (q h) -> p q h", q=QC)
        up_s = (vT, vtok[:, :])
        hidf = conv
        xa_m = gateT[:, :]
        maskb = sqq[:, 0:B]
        rows_flat = rows[:, :, :, :].rearrange("p b q c -> p (b q c)")
        adi = rows_flat[:, 0:B].bitcast(I32)
        adf = rows_flat[:, B:2 * B]
        outs = qkT[:, 1, :, :].rearrange("p b n -> p (b n)").rearrange("p (q o) -> p q o", o=HID)

        waits_stood = sem("waits_stood")

        STEPS = T - 1
        LAST_SPLIT = 15
        BEFORE_STEPS = 1 + 8 + 2 + 2 + 1 + 3 * 2
        N_PARTS = BEFORE_STEPS + 2 * STEPS + 1

        split_below = {0: T, NKH - 1: LAST_SPLIT}

        def leave(eng, v0, heads, r):
            n = T - r
            vs = slice(v0, v0 + heads)
            tmp0 = v0 * T * T // 4
            tmp = step_tmp[:, tmp0:tmp0 + heads * r * n].rearrange("p (v s t) -> p v s t", v=heads, s=r)
            rows_ = mix[:, vs, 0:r, r:T]
            return (lambda: eng.tensor_tensor(tmp, dec[:, vs, 0:r, r].unsqueeze(3).broadcast_to([P, heads, r, n]),
                                              mix[:, vs, r, r:T].unsqueeze(2).broadcast_to([P, heads, r, n]), ALU.mult),
                    lambda: eng.tensor_tensor(rows_, rows_, tmp, ALU.subtract))

        TH = T // 2
        prods_kq = prods[:, :, 0:2 * T].rearrange("p s (a t) -> p s a t", a=2)

        def region(h):
            return slice(h * TH, (h + 1) * TH), slice(h * TH, T), T - h * TH

        def start_at_one(eng, *sems):
            for s in sems:
                eng.sem_inc(s, 1)

        def alone(eng):
            eng.sem_inc(waits_stood, 1)

        block = ctx.enter_context(nc.Block())

        @block.sync
        def _(sp):
            sp.dma_start(idx[:, 0:1], itok_set).then_inc(ld_idx, 16)
            for dst, src in ((ident[:, :], ident_in), (nw[:, :], norm_w),
                             (small[0:2 * NVH, 0:2], gate_col)):
                sp.dma_start(dst, src).then_inc(ld_const, 16)
            sp.dma_start(wab_in, w_ab).then_inc(ld_const, 16)
            sp.dma_start(wqk_in[:, :], w_qk[0]).then_inc(ld_wqk, 16)
            sp.wait_ge(ld_gath, 16)
            sp.dma_start(gathered_d, gath).then_inc(st_gath, 16)
            sp.wait_ge(st_gath, 16)
            sp.dma_start(cw, gathered_d.rearrange("(q b) (c d) -> (b c) q d", b=QB, d=T)).then_inc(ld_cw, 16)
            xq = x.rearrange("(g q b) c h -> g (b c) q h", q=QC, b=QB)
            for p in range(2):
                sp.dma_start(xs[:, p], xq[p]).then_inc(ld_xs[p], 16)
            for g in range(2, NCH):
                sp.wait_ge(cond_mm, g - 1)
                sp.dma_start(xs[:, g % 2], xq[g]).then_inc(ld_xs[g % 2], 16)
            sp.wait_ge(wab_split, 1)
            sp.dma_start(wvz_in[:, :], w_vz[0]).then_inc(ld_wvz, 16)
            sp.dma_start(wo_in[:, :], w_o[0]).then_inc(ld_wo, 16)
            sp.wait_ge(wqk_ready, 1)
            sp.dma_start(wqk_in[:, :], w_qk[1]).then_inc(ld_wqk, 16)
            sp.wait_ge(g_dve, 4)
            sp.dma_start(gates_d[0:NVH], graw[0:NVH]).then_inc(st_gates, 16)
            sp.wait_ge(st_gates, 16)
            sp.dma_start(gsum[0], gates_d[0:NVH].rearrange("h (b t) -> b h t", t=T)).then_inc(ld_gates, 16)
            sp.wait_ge(g_sum, 5)
            sp.dma_start(cums_d, gsum[1]).then_inc(st_cums, 16)
            beta_v = gates_d[NVH:2 * NVH].rearrange("(k v) (b t) -> k b v t", v=NV, t=T)
            cums_v = cums_d.rearrange("b (k v) t -> k b v t", v=NV)

            def load_decays(kk):
                sp.dma_start(gk[:, 0], cums_v[kk]).then_inc(ld_cums, 16)

            def load_betas(kk):
                sp.dma_start(gk[:, 1], beta_v[kk]).then_inc(ld_betas, 16)

            def products(w0):
                for p in range(2):
                    sp.wait_ge(st_prods[p], (w0 + NCH) * 8 + 16)

            def load_prods(kk):
                sp.dma_start(solve[:, 0:T * RW],
                             prods_d[kk].rearrange("b t w -> b (t w)")).then_inc(ld_prods, 16)

            def store_mix(kk):
                sp.wait_ge(mix_ready, kk + 1)
                sp.dma_start(mix_d[kk].rearrange("b v s t -> b (v s t)"),
                             solve[:, X0:X0 + NV * T * T]).then_inc(st_mix, 16)

            def load_mix(kk):
                sp.wait_ge(st_mix, (kk + 1) * 16)
                src = mix_d[kk].rearrange("(q b) v s t -> b v s q t", b=QB)
                for b in range(QB):
                    for v in range(NV):
                        sp.dma_start(mixT[32 * b:32 * b + 32, v, :, 32 * b:32 * b + 32],
                                     src[b, v]).then_inc(ld_mix, 16)

            def load_vz(kk):
                sp.wait_ge(wvz_ready, kk)
                sp.wait_ge(wo_ready, kk)
                sp.dma_start(wvz_in[:, :], w_vz[kk]).then_inc(ld_wvz, 16)
                sp.dma_start(wo_in[:, :], w_o[kk]).then_inc(ld_wo, 16)

            sp.wait_ge(st_cums, 16)
            load_decays(0)
            sp.wait_ge(diff_ready, 1)
            load_decays(1)
            sp.wait_ge(betas_act, 1)
            sp.dma_start(gates_d[NVH:2 * NVH], graw[NVH:2 * NVH]).then_inc(st_betas, 16)
            products(0)
            load_prods(0)
            sp.wait_ge(st_betas, 16)
            load_betas(0)
            sp.dma_start(acc[:, :, :], x.rearrange("(q b) c h -> (b c) q h", b=QB)).then_inc(ld_x, 16)
            store_mix(0)
            sp.wait_ge(zero_mix, 1)
            load_mix(0)
            products(NCH)
            load_prods(1)
            load_betas(1)
            with sp.Fori(0, NKH - 2) as i:
                sp.wait_ge(wqk_ready, i + 2)
                alone(sp)
                sp.dma_start(wqk_in[:, :], w_qk[i + 2]).then_inc(ld_wqk, 16)
                load_vz(i + 1)
                sp.wait_ge(diff_ready, i + 2)
                load_decays(i + 2)
                store_mix(i + 1)
                sp.wait_ge(o_mm, (i + 1) * NU + 1)
                alone(sp)
                load_mix(i + 1)
                products((i + 2) * NCH)
                load_prods(i + 2)
                load_betas(i + 2)
            load_vz(NKH - 1)
            store_mix(NKH - 1)
            sp.wait_ge(o_mm, (NKH - 1) * NU + 1)
            load_mix(NKH - 1)
            sp.wait_ge(wqk_ready, NKH)
            sp.wait_ge(wvz_ready, NKH)
            sp.wait_ge(wo_ready, NKH)
            for dst, src in ((w1_in, w1), (w3_in, w3), (w2_in, w2), (lw_in, lora_w), (la_in, lora_a),
                             (lb_in, lora_b), (hads, had), (adi, itok_ad.partition_broadcast(P)),
                             (small[:, 2:3], scal_col), (small[:, 3:4], ad_col)):
                sp.dma_start(dst, src).then_inc(ld_ffn, 16)
            outq = out.rearrange("(c q b) t h -> c (b t) q h", q=QC, b=QB)
            with sp.Fori(0, NCH) as c:
                sp.wait_ge(ff_add, c + 2)
                sp.dma_start(outq[c], outs).then_inc(st_out, 16)
            sp.wait_ge(st_out, 16 * NCH)

        @block.gpsimd
        def _(pool):
            pool.wait_ge(ld_idx, 16)
            pool.indirect_dma_start(gath, None, cond_w,
                                    bass.IndirectOffsetOnAxis(ap=idx[:, 0:1].bitcast(U32), axis=0)).then_inc(ld_gath, 16)
            pool.memset(cw_blk, 0.0).then_inc(zero_cw, 1)
            pool.memset(ones[:, :], 1.0)
            pool.memset(half[:, :], -0.5)
            pool.memset(rows[:, :, :, :], 0.0).then_inc(consts_set, 1)

            def split(hi, lo, full, ready, n_hi):
                pool.tensor_copy(hi, full).then_inc(solve_chain, 1)
                pool.wait_ge(solve_chain, n_hi)
                pool.tensor_tensor(lo, full, hi.bitcast(F32), ALU.subtract).then_inc(ready, 1)

            wab_hi = wvz_hi[:, 0:KH, :]
            wab_lo = wvz_lo[:, 0:KH, :]
            pool.wait_ge(ld_const, 16 * 4)
            split(wab_hi, wab_lo, wab_in, wab_split, 1)

            SLOT_ROOM, FIRST_ROOM, POW_ROOM = 2000, 1000, 600

            def qk_rest(n):
                pool.wait_ge(wqk_high, n + 1)
                pool.tensor_tensor(wqk_lo[:, :, :], wqk_in[:, 0:4 * P].rearrange("p (a b) -> p a b", a=4),
                                   wqk_hi[:, :, :].bitcast(F32), ALU.subtract).then_inc(wqk_ready, 1)

            def vz_rest(n):
                pool.wait_ge(wvz_high, n + 1)
                pool.tensor_tensor(wvz_lo[:, :, :], wvz_in[:, 0:8 * P].rearrange("p (a b) -> p a b", a=8),
                                   wvz_hi[:, :, :].bitcast(F32), ALU.subtract).then_inc(wvz_ready, 1)

            qk_rest(0)
            pool.memset(mixf, 0.0).then_inc(zero_mix, 1)
            pool.wait_ge(cond_mm, NCH)
            pool.memset(mix[:, :, :, :], 0.0)
            pool.wait_ge(ld_gates, 16)
            for n, sh in enumerate((1, 2, 4, 8, 16)):
                a, b = gsum[n % 2], gsum[(n + 1) % 2]
                if n:
                    pool.wait_ge(g_sum, n)
                pool.tensor_copy(b[:, :, 0:sh], a[:, :, 0:sh])
                pool.tensor_tensor(b[:, :, sh:T], a[:, :, sh:T], a[:, :, 0:T - sh], ALU.add).then_inc(g_sum, 1)

            def solve_parts(kk, base):
                done = [base]
                split_at = split_below.get(kk, 0) if isinstance(kk, int) else 0

                def link(ins):
                    ins.then_inc(solve_chain, 1)
                    done[0] += 1

                def after():
                    pool.wait_ge(solve_chain, done[0])

                def norms():
                    pool.wait_ge(ld_prods, (kk + 1) * 16)
                    alone(pool)
                    flat = solve[:, 0:T * RW]
                    diag = flat[:, 0:(T - 1) * (RW + 1) + 1:RW + 1]
                    pool.tensor_scalar(inv_norm[:, 0, :], diag, 1e-24, None, ALU.max)
                    link(pool.tensor_scalar(inv_norm[:, 1, :], prods[:, :, 2 * T], 1e-24, None, ALU.max))

                def norm_powers(n):
                    after()
                    iv = inv_norm[:, :, :].rearrange("p a t -> p (a t)")[:, n * T // 4:(n + 1) * T // 4]
                    link(pool.tensor_tensor(iv, iv, half[:, 0:T // 4], ALU.pow))

                def scale_rows(h):
                    after()
                    r, c, w = region(h)
                    p = prods_kq[:, r, :, c]
                    link(pool.tensor_tensor(p, p, inv_norm[:, 0, r].unsqueeze(2).unsqueeze(3).broadcast_to([P, TH, 2, w]),
                                            ALU.mult))

                def scale_cols(h):
                    after()
                    r, c, w = region(h)
                    p = prods_kq[:, r, :, c]
                    link(pool.tensor_tensor(p, p, inv_norm[:, :, c].unsqueeze(1).broadcast_to([P, TH, 2, w]), ALU.mult))

                def causal():
                    after()
                    alone(pool)
                    for h in range(2):
                        b = prods_kq[:, h * TH:(h + 1) * TH, 1, h * TH:(h + 1) * TH]
                        last = pool.affine_select(out=b, in_=b, compare_op=ALU.is_ge, fill=0.0, base=0,
                                                  pattern=[[-1, TH], [1, TH]], channel_multiplier=0)
                    link(last)

                def decay_q(h):
                    after()
                    if h == 0:
                        pool.wait_ge(dec_ready, kk + 1)
                        if_first_store(kk)
                    r, c, w = region(h)
                    link(pool.tensor_tensor(mix[:, :, r, c], dec[:, :, r, c],
                                            prods_kq[:, r, 1, c].unsqueeze(1).broadcast_to([P, NV, TH, w]), ALU.mult))

                def decay_k(h):
                    after()
                    r, c, w = region(h)
                    link(pool.tensor_tensor(dec[:, :, r, c], dec[:, :, r, c],
                                            prods_kq[:, r, 0, c].unsqueeze(1).broadcast_to([P, NV, TH, w]), ALU.mult))

                def beta_k(h):
                    if h == 0:
                        pool.wait_ge(ld_betas, (kk + 1) * 16)
                    after()
                    r, c, w = region(h)
                    link(pool.tensor_tensor(dec[:, :, r, c], dec[:, :, r, c],
                                            gk[:, 1, :, c].unsqueeze(2).broadcast_to([P, NV, TH, w]), ALU.mult))

                def step(r):
                    after()
                    prod, rest = leave(pool, 0, NV - 1 if r < split_at else NV, r)
                    link(prod())
                    after()
                    link(rest())

                def beta_out(h):
                    after()
                    if split_at and h == 0:
                        pool.wait_ge(dve_steps, 2 * (T - 1) + (0 if kk == 0 else 2 * (split_at - 1)))
                    r, c, w = region(h)
                    ins = pool.tensor_tensor(mix[:, :, r, c], mix[:, :, r, c],
                                             gk[:, 1, :, r].unsqueeze(3).broadcast_to([P, NV, TH, w]), ALU.mult)
                    if h == 1:
                        ins.then_inc(mix_ready, 1)
                    else:
                        link(ins)

                def if_first_store(kk_):
                    if not (isinstance(kk_, int) and kk_ == 0):
                        pool.wait_ge(st_mix, kk_ * 16)

                size = (2 * TH * T, 2 * TH * TH)
                return ([(norms, 100)]
                        + [(lambda n=n: norm_powers(n), POW_ROOM) for n in range(8)]
                        + [(lambda f=f, h=h: f(h), size[h]) for f in (scale_rows, scale_cols) for h in range(2)]
                        + [(causal, 2 * TH * TH)]
                        + [(lambda f=f, h=h: f(h), size[h]) for f in (decay_q, decay_k, beta_k) for h in range(2)]
                        + [(lambda r=r: step(r), 2 * NV * r * (T - r) + 80) for r in range(T - 1, 0, -1)]
                        + [(lambda h=h: beta_out(h), size[h]) for h in range(2)])

            def differences(kk):
                pool.wait_ge(ld_cums, (kk + 1) * 16)
                if not (isinstance(kk, int) and kk == 0):
                    pool.wait_ge(mix_ready, kk)
                g = gk[:, 0]
                for h in range(2):
                    r, c, w = region(h)
                    last = pool.tensor_tensor(dec[:, :, r, c], g[:, :, c].unsqueeze(2).broadcast_to([P, NV, TH, w]),
                                              g[:, :, r].unsqueeze(3).broadcast_to([P, NV, TH, w]), ALU.subtract)
                last.then_inc(diff_chain, 1)
                pool.wait_ge(diff_chain, kk + 1)
                alone(pool)
                for h in range(2):
                    r, c, w = region(h)
                    last = pool.tensor_scalar(dec[:, :, r, c], dec[:, :, r, c], 0.0, None, ALU.min)
                last.then_inc(diff_ready, 1)

            def rstd_of(u, par):
                pool.wait_ge(ms_ready, u + 1)
                pool.tensor_tensor(rstd[:, par, :], ms[:, par, :], half[:, 0:QC], ALU.pow).then_inc(rstd_ready, 1)

            differences(0)
            qk_rest(1)
            vz_rest(0)
            for piece, _ in solve_parts(0, 1):
                piece()
            differences(1)

            def norms_and_solve(i, more_qk):
                parts = solve_parts(i + 1, i * N_PARTS + (1 + N_PARTS))
                for j in range(NU + 1):
                    if j == NU - 1 and more_qk:
                        qk_rest(i + 2)
                    if j:
                        rstd_of(i * NU + (j - 1), (j - 1) % 2)
                    room = SLOT_ROOM if j else FIRST_ROOM
                    while parts and room >= parts[0][1] // 2:
                        piece, n = parts.pop(0)
                        piece()
                        room -= n
                for piece, _ in parts:
                    piece()
                vz_rest(i + 1)

            with pool.Fori(0, NKH - 2) as i:
                norms_and_solve(i, True)
                differences(i + 2)
            norms_and_solve(NKH - 2, False)

            w13 = [(w[:, k], [h[:, k] for h in hs]) for w, hs in ((w1_in, w1h), (w3_in, w3h)) for k in range(KH)]
            lora = ((lw_in, lwh), (la_in, lah), (lb_in, lbh))

            def w13_high(n):
                if n == 0:
                    pool.wait_ge(ld_ffn, 16 * 10)
                    pool.wait_ge(z_mm, (NKH - 1) * NU + NU // 2)
                pool.tensor_copy(w13[n][1][0], w13[n][0]).then_inc(w_high, 1)

            def w13_low(n):
                pool.wait_ge(w_high, 2 * KH)
                pool.tensor_tensor(w13[n][1][1], w13[n][0], w13[n][1][0].bitcast(F32), ALU.subtract).then_inc(w_low, 1)

            def lora_highs():
                pool.wait_ge(z_mm, (NKH - 1) * NU + NU // 2 + NV)
                for w, h in lora:
                    last = pool.tensor_copy(h[0], w)
                last.then_inc(lora_high, 1)

            def lora_lows():
                pool.wait_ge(lora_high, 1)
                for w, h in lora:
                    last = pool.tensor_tensor(h[1], w, h[0].bitcast(F32), ALU.subtract)
                last.then_inc(lora_low, 1)

            splits = ([lambda n=n: w13_high(n) for n in range(2 * KH)] + [lambda n=n: w13_low(n) for n in range(2 * KH)]
                      + [lora_highs, lora_lows])
            for j in range(NU):
                rstd_of((NKH - 1) * NU + j, j % 2)
                if j >= NU // 2 and splits:
                    for _ in range(2 if len(splits) > NU - 1 - j else 1):
                        splits.pop(0)()

            pool.wait_ge(acc_done, NKH * NU + 1)

            def x1_chunk(c):
                pool.tensor_copy(x1c, acc[:, bass.ds(c * QC, QC), :]).then_inc(x1_copy, 1)

            def hid_rest(c):
                for m in range(FT):
                    pool.wait_ge(hid_high, c * FT + (m + 1))
                    pool.tensor_tensor(hidh[1][:, m, :], hidf[:, m % 2, :], hidh[0][:, m, :].bitcast(F32),
                                       ALU.subtract).then_inc(hid_low, 1)

            x1_chunk(0)
            with pool.Fori(0, NCH - 1) as c:
                pool.wait_ge(x1_tr, c * KH + KH)
                alone(pool)
                x1_chunk(c + 1)
                hid_rest(c)
            hid_rest(NCH - 1)

        @block.tensor
        def _(pe):
            start_at_one(pe, v_tr, o_mm, out_mm)

            def three(ps, hi, lo, k0, cols):
                n = 0
                for k in range(KH):
                    for w, m in ((hi, xhi), (lo, xhi), (hi, xlo)):
                        mm = pe.matmul(ps, w[:, k0 + k, :], m[:, k, cols], start=(n == 0), stop=(n == 3 * KH - 1))
                        n += 1
                return mm

            pe.wait_ge(zero_cw, 2)
            for g in range(NCH):
                pe.wait_ge(ld_xs[g % 2], 16 * (g // 2 + 1))
                if g >= 2:
                    pe.wait_ge(cond_hi, g - 1)
                    pe.wait_ge(cond_lo, g - 1)
                for k in range(KH):
                    for q in range(QC):
                        mm = pe.matmul(qk_banks[g % 2][k][:, q * P:(q + 1) * P], xs[:, g % 2, q, k * P:(k + 1) * P],
                                       cw_blk[:, g * QC + q, :], start=True, stop=True)
                mm.then_inc(cond_mm, 1)
            pe.wait_ge(wab_split, 1)
            pe.wait_ge(cond_lo, NCH)
            pe.wait_ge(cond_hi, NCH)
            with pe.Fori(0, NCH // 2) as g2:
                for p, ps in ((0, psR), (1, psS)):
                    g = g2 * 2 + p
                    n = 0
                    pe.wait_ge(gate_ev, g2 * 2 + p + 1)
                    three(ps[:, :], wvz_hi, wvz_lo, 0, bass.ds(g2 * (2 * CH) + p * CH, CH)).then_inc(gate_mm, 1)

            def qk_proj(w, par, c, first):
                for a, bank_, conv_done, mm_done in ((0, qk_banks[par][0], q_conv, q_mm),
                                                     (1, qk_banks[par][1], k_conv, k_mm)):
                    if not first:
                        pe.wait_ge(conv_done, w - 1)
                    three(bank_[:, :], wqk_hi, wqk_lo, KH * a, bass.ds(c, CH)).then_inc(mm_done, 1)

            def prods_of(w, par):
                pe.wait_ge(q_ready, w + 1)
                pe.wait_ge(k_ready, w + 1)
                pe.wait_ge(rows_ev, w + 1)
                for q in range(QC):
                    for b in range(QB):
                        t0 = q * P + b * T
                        pe.matmul(psRv[b * T:(b + 1) * T, q, 0:2 * T], qkT[:, par, 0, t0:t0 + T],
                                  qkT[:, par, :, t0:t0 + T], start=True, stop=True)
                pe.wait_ge(q_sq, w + 1)
                for q in range(QC):
                    mm = pe.matmul(psRv[:, q, 2 * T:2 * T + 1], sqq[:, q * P:(q + 1) * P], ones[:, 0:1],
                                   start=True, stop=True)
                mm.then_inc(prod_mm, 1)

            def stage1(w0, first, v_head=None):
                qk_proj(w0 + 1, 1, CH, first)
                with pe.Fori(0, NCH // 2 - 1) as c2:
                    for p in range(2):
                        w = c2 * 2 + (w0 + p)
                        qk_proj(w + 2, p, c2 * (2 * CH) + (p + 2) * CH, False)
                        prods_of(w, p)
                if v_head is not None:
                    pe.wait_ge(wvz_ready, v_head + 1)
                    pe.wait_ge(q_conv, w0 + (NCH - 1))
                    v_proj(v_head * NU, 0, 0)
                prods_of(w0 + (NCH - 2), 0)
                prods_of(w0 + (NCH - 1), 1)

            def v_proj(u, v, c):
                pe.wait_ge(v_conv, u + 1)
                three(psA[:, :], wvz_hi, wvz_lo, 4 * v, bass.ds(c, CH)).then_inc(v_mm, 1)

            def z_proj(u, v, c):
                pe.wait_ge(z_ready, u + 1)
                three(psB[:, :], wvz_hi, wvz_lo, 4 * v + 2, bass.ds(c, CH)).then_inc(z_mm, 1)

            def turn_v(u):
                pe.wait_ge(v_ready, u + 1 + 1)
                pe.wait_ge(v_tok, u + 1)
                for q in range(QC):
                    mm = pe.transpose(psT[:, q * P:(q + 1) * P], vT[:, q * P:(q + 1) * P], ident[:, :])
                mm.then_inc(v_tr, 1)

            def apply_mix(u, v, c):
                pe.wait_ge(v_tok, u + 1 + 1)
                pe.wait_ge(y_ready, u + 1)
                for q in range(QC):
                    mm = pe.matmul(psO[:, q * P:(q + 1) * P], vtok[:, q * P:(q + 1) * P],
                                   mixf[:, bass.ds(v * (NQUAD * P) + c + q * P, P)], start=True, stop=True)
                mm.then_inc(o_mm, 1)

            def out_proj(u, v, par):
                pe.wait_ge(y_sq, u + 1)
                pe.wait_ge(acc_done, u + 1)
                pe.wait_ge(y_low, u + 2)
                for q in range(QC):
                    pe.matmul(psS[:, q:q + 1], ysq[:, q * P:(q + 1) * P], ones[:, 0:1], start=True, stop=True)
                for q in range(QC):
                    cols = slice(q * P, (q + 1) * P)
                    for n, (y, w) in enumerate(((y_hi[par], wo_hi), (y_lo[par], wo_hi), (y_hi[par], wo_lo))):
                        mm = pe.matmul(psWv[:, q, :], y[:, cols], w[:, v, :], start=(n == 0), stop=(n == 2))
                mm.then_inc(out_mm, 1)

            def stage2(i, more_qk):
                u0 = i * NU

                def slot(u, c, k, head, last):
                    if head:
                        pe.wait_ge(wo_ready, i + 1)
                        z_proj(u, k % 2, c)
                        turn_v(u)
                    if not last:
                        v_proj(u + 1, (k + 1) % 2, c + (CH if k % 2 else 0))
                    if not head:
                        turn_v(u)
                    if head:
                        pe.wait_ge(ld_mix, (i + 1) * (16 * QB * NV))
                    else:
                        z_proj(u, k % 2, c)
                    apply_mix(u, k % 2, c)
                    if not head:
                        out_proj(u - 1, (k + 1) % 2, (k + 1) % 2)

                slot(u0, 0, 0, True, False)
                slot(u0 + 1, 0, 1, False, False)
                with pe.Fori(1, NCH - 1) as c:
                    for k in range(2):
                        slot(u0 + c * 2 + k, c * CH, k, False, False)
                slot(u0 + (NU - 2), (NCH - 1) * CH, 0, False, False)
                slot(u0 + (NU - 1), (NCH - 1) * CH, 1, False, True)
                if more_qk:
                    pe.wait_ge(wqk_ready, i + 3)
                    pe.wait_ge(z_ready, u0 + (NU + 1))
                    qk_proj(i * NCH + 2 * NCH, 0, 0, False)
                out_proj(u0 + (NU - 1), 1, 1)

            pe.wait_ge(wqk_ready, 1)
            qk_proj(0, 0, 0, True)
            stage1(0, True)
            pe.wait_ge(wqk_ready, 2)
            qk_proj(NCH, 0, 0, False)
            stage1(NCH, False, 0)
            with pe.Fori(0, NKH - 2) as i:
                stage2(i, True)
                stage1(i * NCH + 2 * NCH, False, i + 1)
            stage2(NKH - 2, False)
            pe.wait_ge(wvz_ready, NKH)
            v_proj((NKH - 1) * NU, 0, 0)
            stage2(NKH - 1, False)

            pe.wait_ge(ld_ffn, 16 * 10)
            for j in range(FT):
                if j >= 2:
                    pe.wait_ge(had_ev, j - 1)
                pe.matmul((psA, psB)[j % 2][:, 0:HID], hads, w2_in[:, j, :], start=True, stop=True).then_inc(had_mm, 1)

            def three_of(ps, w, m, first=True, last=True):
                n, end = 0, 3 * len(w) - 1
                for a, b in zip(w, m):
                    for x_, y_ in ((0, 0), (1, 0), (0, 1)):
                        mm = pe.matmul(ps, a[x_], b[y_], start=(first and n == 0), stop=(last and n == end))
                        n += 1
                return mm

            def turn_x1(c, first):
                pe.wait_ge(x1_copy, c + 1)
                for k, ps in ((0, psT), (1, psO)):
                    if not first:
                        pe.wait_ge(xa_f, c) if k == 0 else pe.wait_ge(x1_low, c * KH)
                    for q in range(QC):
                        mm = pe.transpose(ps[:, q * P:(q + 1) * P], x1c[:, q, k * P:(k + 1) * P], ident[:, :])
                    mm.then_inc(x1_tr, 1)

            def adapters_in(c):
                pe.wait_ge(lora_low, 1)
                pe.wait_ge(x1_low, c * KH + KH)
                three_of(psT[:, :], [[h[:, k, :] for h in lah] for k in range(KH)],
                         [[h[:, k, :] for h in x1h] for k in range(KH)]).then_inc(xa_mm, 1)

            def h_out(c, first):
                pe.wait_ge(xa_low, c + 1)
                if first:
                    pe.wait_ge(had_ev, FT)
                else:
                    pe.wait_ge(hid_f, c * FT)
                for o, ps in ((0, psA), (1, psB)):
                    cols = slice(o * P, (o + 1) * P)
                    mm = three_of(ps[:, :], [[h[:, k, cols] for h in lwh] for k in range(KH)] + [[h[:, cols] for h in lbh]],
                                  [[h[:, k, :] for h in x1h] for k in range(KH)] + [xah])
                mm.then_inc(h_mm, 1)

            def up_and_lin(c):
                pe.wait_ge(w_low, 2 * KH)
                pe.wait_ge(h_low, c * KH + KH)
                for m in range(FT):
                    cols = slice(m * P, (m + 1) * P)
                    if m >= 2:
                        pe.wait_ge(hid_f, c * FT + (m - 1))
                    for ps, w, done in (((psA, psR)[m % 2], w1h, up_mm), ((psB, psS)[m % 2], w3h, lin_mm)):
                        three_of(ps[:, :], [[h[:, k, cols] for h in w] for k in range(KH)],
                                 [[h[:, k, :] for h in hTh] for k in range(KH)]).then_inc(done, 1)

            def down(c, quads):
                if quads[0] == 0:
                    pe.wait_ge(w2_ready, 2)
                    pe.wait_ge(hid_low, c * FT + FT)
                    pe.wait_ge(ff_add, c + 1)
                for q in quads:
                    mm = three_of(psWv[:, q, :], [[h[:, m, q * P:(q + 1) * P] for h in hidh] for m in range(FT)],
                                  [[h[:, m, :] for h in w2h] for m in range(FT)])
                if quads[-1] == QC - 1:
                    mm.then_inc(ff_mm, 1)

            turn_x1(0, True)
            adapters_in(0)
            h_out(0, True)
            with pe.Fori(0, NCH - 1) as c:
                turn_x1(c + 1, False)
                up_and_lin(c)
                adapters_in(c + 1)
                down(c, (0, 1))
                h_out(c + 1, False)
                down(c, (2, 3))
            up_and_lin(NCH - 1)
            down(NCH - 1, (0, 1))
            down(NCH - 1, (2, 3))

        @block.scalar
        def _(act):
            start_at_one(act, z_ready, v_tok, v_ready, rows_ev)
            for s in st_prods:
                act.sem_inc(s, 16)

            def qk_high(n):
                act.wait_ge(ld_wqk, (n + 1) * 16)
                act.activation(taps_qk[:, :, :], wqk_in[:, 4 * P:4 * P + 8].rearrange("p (a b) -> p a b", a=2), ACT.Copy)
                act.activation(wqk_hi[:, :, :], wqk_in[:, 0:4 * P].rearrange("p (a b) -> p a b", a=4),
                               ACT.Copy).then_inc(wqk_high, 1)

            for g in range(NCH):
                act.wait_ge(cond_mm, g + 1)
                for k in range(KH):
                    last = act.activation(xhi[:, k, g * CH:(g + 1) * CH], qk_banks[g % 2][k][:, :], ACT.Copy)
                last.then_inc(cond_hi, 1)
            qk_high(0)
            act.wait_ge(ld_cw, 16)
            for g in range(NCH):
                if g == 0:
                    act.activation(small[0:1, 6:7], small[0:1, 0:1], ACT.Copy).then_inc(gate_ev, 1)
                act.wait_ge(gate_mm, g + 1) if g else None
                ps = (psR, psS)[g % 2]
                if g == 0:
                    act.activation(small[0:1, 5:6], small[0:1, 0:1], ACT.Copy).then_inc(gate_ev, 1)
                    act.wait_ge(gate_mm, 1)
                act.activation(graw[:, g * CH:(g + 1) * CH], ps[0:2 * NVH, :], ACT.Copy).then_inc(gate_ev, 1)
            a_rows = graw[0:NVH]
            b_rows = graw[NVH:2 * NVH]
            act.wait_ge(gate_ev, NCH + 2)
            act.activation(small[0:NVH, 4:5], small[0:NVH, 1:2], ACT.Exp).then_inc(g_act, 1)
            act.wait_ge(g_dve, 1)
            act.activation(gtmp[0:NVH], gtmp[0:NVH], ACT.Exp, scale=-1.0).then_inc(g_act, 1)
            act.wait_ge(g_act, 2)
            act.activation(gtmp[0:NVH], gtmp[0:NVH], ACT.Ln, bias=1.0).then_inc(g_act, 1)

            def tap_qk(w, par, first=False):
                for a, mm, tap, rd in ((0, q_mm, q_tap, q_ready), (1, k_mm, k_tap, k_ready)):
                    act.wait_ge(mm, w + 1)
                    if not first:
                        act.wait_ge(rd, w - 1)
                    act.activation(qk_conv[par][a], qk_banks[par][a][:, :], ACT.Copy,
                                   scale=taps_qk[:, a, TAPS - 1:TAPS]).then_inc(tap, 1)

            def silu_qk(w, par, first):
                if not first:
                    act.wait_ge(prod_mm, w - 1)
                for a, cv, rd in ((0, q_conv, q_ready), (1, k_conv, k_ready)):
                    act.wait_ge(cv, w + 1)
                    act.activation(qkT[:, par, 1 - a, :], qk_conv[par][a], ACT.Silu).then_inc(rd, 1)

            def square_q(w, par):
                act.wait_ge(q_ready, w + 1)
                act.activation(sqq[:, :], qkT[:, par, 1, :], ACT.Square).then_inc(q_sq, 1)

            rows_d = prods_d.rearrange("k (c q b) t w -> (k c) (b t) q w", q=QC, b=QB)

            def rows_out(w, par, first):
                act.wait_ge(prod_mm, w + 1)
                if not first:
                    act.wait_ge(st_prods[par], (w - par) * 8 + 16)
                act.activation(rows[:, par, :, 0:2 * T + 1], psRv[:, :, 0:2 * T + 1], ACT.Copy).then_inc(rows_ev, 1)
                act.wait_ge(rows_ev, w + 2)
                act.dma_start(rows_d[w], rows[:, par]).then_inc(st_prods[par], 16)

            def stage1(w0, first, v_head=None, new_vz=False):
                tap_qk(w0, 0, first)
                tap_qk(w0 + 1, 1, first)
                if new_vz:
                    act.wait_ge(out_mm, v_head * NU + 1)
                    vz_high(v_head)
                silu_qk(w0, 0, first)
                square_q(w0, 0)
                tap_qk(w0 + 2, 0)
                silu_qk(w0 + 1, 1, first)
                rows_out(w0, 0, first)
                square_q(w0 + 1, 1)
                tap_qk(w0 + 3, 1)
                with act.Fori(1, NCH // 2 - 1) as c2:
                    for p in range(2):
                        w = c2 * 2 + (w0 + p)
                        silu_qk(w, p, False)
                        rows_out(w - 1, 1 - p, False)
                        square_q(w, p)
                        tap_qk(w + 2, p)
                for p in range(2):
                    w = w0 + (NCH - 2 + p)
                    silu_qk(w, p, False)
                    rows_out(w - 1, 1 - p, False)
                    square_q(w, p)
                    if v_head is not None and p == 0:
                        tap_v(v_head * NU, 0)
                if v_head is not None:
                    silu_v(v_head * NU)
                rows_out(w0 + (NCH - 1), 1, False)
                if v_head is not None:
                    decay_exp(v_head + 1)

            def tap_v(u, v):
                act.wait_ge(v_mm, u + 1)
                act.wait_ge(v_ready, u + 1)
                act.activation(conv[:, 0, :], psA[:, :], ACT.Copy, scale=taps_v[:, v, TAPS - 1:TAPS]).then_inc(v_tap, 1)

            def silu_v(u):
                act.wait_ge(v_conv, u + 1 + 1)
                act.wait_ge(v_tr, u + 1)
                act.activation(vT, conv[:, 0, :], ACT.Silu).then_inc(v_ready, 1)

            def stage2(i, more_qk):
                u0 = i * NU

                def slot(u, k, last):
                    act.wait_ge(v_tr, u + 1 + 1)
                    act.wait_ge(o_mm, u + 1)
                    act.activation(vtok[:, :], psT[:, :], ACT.Copy).then_inc(v_tok, 1)
                    if not last:
                        tap_v(u + 1, 1 - k)
                    act.wait_ge(z_mm, u + 1)
                    act.wait_ge(y_ready, u + 1)
                    act.activation(gateT[:, :], psB[:, :], ACT.Silu).then_inc(z_ready, 1)
                    if not last:
                        silu_v(u + 1)
                    act.wait_ge(y_ready, u + 1 + 1)
                    act.activation(y_hi[k], yT, ACT.Copy).then_inc(y_high, 1)
                    act.wait_ge(out_mm, u + 1)
                    act.activation(ysq[:, :], yT, ACT.Square).then_inc(y_sq, 1)

                slot(u0, 0, False)
                slot(u0 + 1, 1, False)
                with act.Fori(1, NCH - 1) as c:
                    for k in range(2):
                        slot(u0 + c * 2 + k, k, False)
                if more_qk:
                    qk_high(i + 2)
                slot(u0 + (NU - 2), 0, False)
                slot(u0 + (NU - 1), 1, True)

            def vz_high(n):
                act.wait_ge(ld_wvz, (n + 1) * 16)
                act.wait_ge(ld_wo, (n + 1) * 16)
                act.activation(taps_v[:, :, :], wvz_in[:, 8 * P:8 * P + 8].rearrange("p (a b) -> p a b", a=2), ACT.Copy)
                act.activation(wo_hi[:, :, :], wo_in[:, :].rearrange("p (v o) -> p v o", v=NV), ACT.Copy, scale=nw[:, 0:1])
                act.activation(wvz_hi[:, :, :], wvz_in[:, 0:8 * P].rearrange("p (a b) -> p a b", a=8),
                               ACT.Copy).then_inc(wvz_high, 1)

            def decay_exp(kk):
                act.wait_ge(diff_ready, kk + 1)
                for h in range(2):
                    r, c, _ = region(h)
                    last = act.activation(dec[:, :, r, c], dec[:, :, r, c], ACT.Exp)
                last.then_inc(dec_ready, 1)

            act.wait_ge(consts_set, 1)
            stage1(0, True)
            qk_high(1)
            act.activation(b_rows, b_rows, ACT.Sigmoid).then_inc(betas_act, 1)
            decay_exp(0)
            act.wait_ge(gate_mm, NCH)
            vz_high(0)
            stage1(NCH, False, 0)
            with act.Fori(0, NKH - 2) as i:
                stage2(i, True)
                stage1(i * NCH + 2 * NCH, False, i + 1, True)
            stage2(NKH - 2, False)
            act.wait_ge(out_mm, (NKH - 1) * NU + 1)
            vz_high(NKH - 1)
            tap_v((NKH - 1) * NU, 0)
            silu_v((NKH - 1) * NU)
            stage2(NKH - 1, False)

            for j in range(FT):
                act.wait_ge(had_mm, j + 1)
                if j == 0:
                    act.wait_ge(w_low, 2 * KH)
                act.activation(w2b[:, j, :], (psA, psB)[j % 2][:, 0:HID], ACT.Copy).then_inc(had_ev, 1)

            def x1_highs(c, first):
                for k, ps in ((0, psT), (1, psO)):
                    act.wait_ge(x1_tr, c * KH + (k + 1))
                    if not first:
                        act.wait_ge(h_mm, c)
                    act.activation(x1h[0][:, k, :], ps[:, :], ACT.Copy).then_inc(x1_high, 1)

            def xa_highs(c):
                act.wait_ge(xa_f, c + 1)
                act.activation(xah[0], xa_m, ACT.Copy).then_inc(xa_high, 1)

            def h_highs(c, first):
                for o, ps in ((0, psA), (1, psB)):
                    act.wait_ge(h_mm, c + 1)
                    if not first:
                        act.wait_ge(lin_mm, c * FT)
                    act.activation(hTh[0][:, o, :], ps[:, :], ACT.Copy).then_inc(h_high, 1)

            def up_highs(c, first):
                for m in range(FT + 1):
                    if m < FT:
                        act.wait_ge(up_mm, c * FT + (m + 1))
                        if not (first and m < 2):
                            act.wait_ge(hid_f, c * FT + (m - 1))
                        act.activation(up_s[m % 2], (psA, psR)[m % 2][:, :], ACT.Silu).then_inc(up_act, 1)
                    if m:
                        act.wait_ge(hid_f, c * FT + m)
                        if not first:
                            act.wait_ge(ff_mm, c)
                        act.activation(hidh[0][:, m - 1, :], hidf[:, (m - 1) % 2, :], ACT.Copy).then_inc(hid_high, 1)

            x1_highs(0, True)
            xa_highs(0)
            h_highs(0, True)
            x1_highs(1, False)
            up_highs(0, True)
            xa_highs(1)
            h_highs(1, False)
            with act.Fori(1, NCH - 1) as c:
                x1_highs(c + 1, False)
                up_highs(c, False)
                xa_highs(c + 1)
                h_highs(c + 1, False)
            up_highs(NCH - 1, False)

        @block.vector
        def _(dve):
            start_at_one(dve, v_conv, y_ready, acc_done, y_low)

            dve.wait_ge(zero_cw, 1)
            dve.wait_ge(ld_cw, 16)
            for b in range(QB):
                last = dve.tensor_copy(cw_blk[32 * b:32 * b + 32, :, 32 * b:32 * b + 32], cw[32 * b:32 * b + 32, :, :])
            last.then_inc(zero_cw, 1)
            for g in range(NCH):
                dve.wait_ge(cond_hi, g + 1)
                for k in range(KH):
                    cols = slice(g * CH, (g + 1) * CH)
                    last = dve.tensor_tensor(xlo[:, k, cols], qk_banks[g % 2][k][:, :], xhi[:, k, cols].bitcast(F32),
                                             ALU.subtract)
                last.then_inc(cond_lo, 1)
            a_rows = graw[0:NVH]
            dve.wait_ge(ld_const, 16 * 4)
            dve.wait_ge(gate_ev, NCH + 2)
            dve.tensor_scalar(a_rows, a_rows, small[0:NVH, 0:1], None, ALU.add).then_inc(v_chain, 1)
            dve.wait_ge(v_chain, 1)
            dve.scalar_tensor_tensor(gtmp[0:NVH], a_rows, -1.0, a_rows, ALU.mult, ALU.max).then_inc(g_dve, 1)
            dve.wait_ge(g_act, 3)
            dve.scalar_tensor_tensor(a_rows, a_rows, 0.0, gtmp[0:NVH], ALU.max, ALU.add).then_inc(g_dve, 1)
            dve.wait_ge(g_dve, 2)
            dve.tensor_scalar(a_rows, a_rows, small[0:NVH, 4:5], -1.0, ALU.mult, ALU.mult).then_inc(g_dve, 1)
            dve.wait_ge(g_dve, 3)
            dve.tensor_copy(small[0:1, 6:7], ones[0:1, 0:1]).then_inc(g_dve, 1)

            def tap(dst, ps, w, j):
                d = dst.rearrange("p (b t) -> p b t", t=T)[:, :, j:T]
                s = ps[:, :].rearrange("p (b t) -> p b t", t=T)[:, :, 0:T - j]
                return dve.scalar_tensor_tensor(d, s, w[:, TAPS - 1 - j:TAPS - j], d, ALU.mult, ALU.add)

            def conv_qk(w, par):
                banks, bufs = qk_banks[par], qk_conv[par]
                for n in range(3):
                    for a in range(2):
                        if n == 0:
                            dve.wait_ge((q_tap, k_tap)[a], w + 1)
                        else:
                            dve.wait_ge(qk_chain, w * 4 + (2 * n - 1 + a))
                        tap(bufs[a], banks[a], taps_qk[:, a, :], n + 1).then_inc(
                            qk_chain if n < 2 else (q_conv, k_conv)[a], 1)

            def conv_v(u, v):
                dve.wait_ge(v_tap, u + 1)
                for j in (1, 2, 3):
                    if j > 1:
                        dve.wait_ge(v_chain, u * 2 + j)
                    ins = tap(conv[:, 0, :], psA, taps_v[:, v, :], j)
                    ins.then_inc(v_chain if j < 3 else v_conv, 1)

            def gate_y(u):
                dve.wait_ge(o_mm, u + 1 + 1)
                dve.wait_ge(z_ready, u + 1 + 1)
                dve.wait_ge(y_low, u + 1)
                dve.tensor_tensor(yT, psO[:, :], gateT[:, :], ALU.mult).then_inc(y_ready, 1)

            def mean_square(u, par):
                dve.wait_ge(out_mm, u + 1 + 1)
                dve.tensor_scalar(ms[:, par, :], psS[:, 0:QC], 1.0 / HD, 1e-6, ALU.mult, ALU.add).then_inc(ms_ready, 1)

            def add_out(u, par, quad):
                dve.wait_ge(rstd_ready, u + 1)
                for q in range(QC):
                    a = acc[:, bass.ds(quad + q, 1), :].rearrange("p q o -> p (q o)")
                    last = dve.scalar_tensor_tensor(a, psWv[:, q, :], rstd[:, par, q:q + 1], a, ALU.mult, ALU.add)
                last.then_inc(acc_done, 1)

            def wo_rest():
                dve.scalar_tensor_tensor(wo_lo[:, :, :], wo_in[:, :].rearrange("p (v o) -> p v o", v=NV), nw[:, 0:1],
                                         wo_hi[:, :, :].bitcast(F32), ALU.mult, ALU.subtract).then_inc(wo_ready, 1)

            def help_solve(kk, done):
                dve.wait_ge(solve_chain, 1 + kk * N_PARTS + BEFORE_STEPS + 2 * (T - split_below[kk]))
                for n, r in enumerate(range(split_below[kk] - 1, 0, -1), start=done):
                    prod, rest = leave(dve, NV - 1, 1, r)
                    if n > done:
                        dve.wait_ge(dve_steps, 2 * n)
                    prod().then_inc(dve_steps, 1)
                    dve.wait_ge(dve_steps, 2 * n + 1)
                    rest().then_inc(dve_steps, 1)

            def stage1(w0, v_head=None, last_out=False):
                conv_qk(w0, 0)
                if last_out:
                    mean_square(v_head * NU - 1, 1)
                conv_qk(w0 + 1, 1)
                if last_out:
                    add_out(v_head * NU - 1, 1, (NCH - 1) * QC)
                with dve.Fori(1, NCH // 2) as c2:
                    for p in range(2):
                        conv_qk(c2 * 2 + (w0 + p), p)
                if v_head is not None:
                    dve.wait_ge(wvz_ready, v_head + 1)
                    wo_rest()
                    conv_v(v_head * NU, 0)

            def stage2(i):
                u0 = i * NU

                def slot(u, k, quad, head, last):
                    if not last:
                        conv_v(u + 1, 1 - k)
                    gate_y(u)
                    if not head:
                        mean_square(u - 1, 1 - k)
                    dve.wait_ge(y_high, u + 1)
                    dve.tensor_tensor(y_lo[k], yT, y_hi[k].bitcast(F32), ALU.subtract).then_inc(y_low, 1)
                    if not head:
                        add_out(u - 1, 1 - k, quad)

                slot(u0, 0, 0, True, False)
                slot(u0 + 1, 1, 0, False, False)
                with dve.Fori(1, NCH - 1) as c:
                    slot(u0 + c * 2, 0, c * QC - QC, False, False)
                    slot(u0 + c * 2 + 1, 1, c * QC, False, False)
                slot(u0 + (NU - 2), 0, (NCH - 2) * QC, False, False)
                slot(u0 + (NU - 1), 1, (NCH - 1) * QC, False, True)

            dve.wait_ge(wqk_ready, 1)
            stage1(0)
            dve.wait_ge(wqk_ready, 2)
            stage1(NCH, 0)
            help_solve(0, 0)
            dve.wait_ge(ld_x, 16)
            with dve.Fori(0, NKH - 2) as i:
                stage2(i)
                dve.wait_ge(wqk_ready, i + 3)
                stage1(i * NCH + 2 * NCH, i + 1, True)
            stage2(NKH - 2)
            mean_square((NKH - 1) * NU - 1, 1)
            add_out((NKH - 1) * NU - 1, 1, (NCH - 1) * QC)
            help_solve(NKH - 1, STEPS)
            dve.wait_ge(wvz_ready, NKH)
            wo_rest()
            conv_v((NKH - 1) * NU, 0)
            stage2(NKH - 1)
            mean_square(NKH * NU - 1, 1)
            add_out(NKH * NU - 1, 1, (NCH - 1) * QC)

            dve.wait_ge(ld_ffn, 16 * 10)
            dve.wait_ge(z_mm, NKH * NU)
            dve.tensor_copy(adf, adi).then_inc(msk, 1)
            dve.wait_ge(msk, 1)
            dve.tensor_scalar(maskb, adf, small[:, 3:4], small[:, 2:3], ALU.is_equal, ALU.mult).then_inc(msk, 1)
            dve.wait_ge(msk, 2)

            def x1_lows(c):
                for k, ps in ((0, psT), (1, psO)):
                    dve.wait_ge(x1_high, c * KH + (k + 1))
                    dve.tensor_tensor(x1h[1][:, k, :], ps[:, :], x1h[0][:, k, :].bitcast(F32),
                                      ALU.subtract).then_inc(x1_low, 1)

            def xa_lows(c, b0):
                dve.wait_ge(xa_mm, c + 1)
                dve.tensor_tensor(xa_m.rearrange("p (b t) -> p b t", t=T), psT[:, :].rearrange("p (b t) -> p b t", t=T),
                                  maskb[:, bass.ds(b0, BC)].unsqueeze(2).broadcast_to([P, BC, T]),
                                  ALU.mult).then_inc(xa_f, 1)
                dve.wait_ge(xa_high, c + 1)
                dve.tensor_tensor(xah[1], xa_m, xah[0].bitcast(F32), ALU.subtract).then_inc(xa_low, 1)

            def h_lows(c):
                for o, ps in ((0, psA), (1, psB)):
                    dve.wait_ge(h_high, c * KH + (o + 1))
                    dve.tensor_tensor(hTh[1][:, o, :], ps[:, :], hTh[0][:, o, :].bitcast(F32),
                                      ALU.subtract).then_inc(h_low, 1)

            def hidden(c, first, between=()):
                for m in range(FT):
                    dve.wait_ge(up_act, c * FT + (m + 1))
                    dve.wait_ge(lin_mm, c * FT + (m + 1))
                    if not (first and m < 2):
                        dve.wait_ge(hid_low, c * FT + (m - 1))
                    dve.tensor_tensor(hidf[:, m % 2, :], (psB, psS)[m % 2][:, :], up_s[m % 2],
                                      ALU.mult).then_inc(hid_f, 1)
                    if m < len(between):
                        between[m]()

            def add_x1(c, quad, first):
                dve.wait_ge(ff_mm, c + 1)
                if not first:
                    dve.wait_ge(st_out, c * 16)
                dve.tensor_tensor(outs, psWv[:, :, :], acc[:, bass.ds(quad, QC), :], ALU.add).then_inc(ff_add, 1)

            x1_lows(0)
            xa_lows(0, 0)
            w2_bufs = (w2b, w2a)

            def butterflies(n):
                r = 1 << n
                dve.wait_ge(had_ev, FT)
                if n:
                    dve.wait_ge(had_add, n)
                s, d = (w.rearrange("p (g two r) o -> p g two (r o)", two=2, r=r)
                        for w in (w2_bufs[n % 2], w2_bufs[(n + 1) % 2]))
                dve.tensor_tensor(d[:, :, 0, :], s[:, :, 0, :], s[:, :, 1, :], ALU.add)
                dve.tensor_tensor(d[:, :, 1, :], s[:, :, 0, :], s[:, :, 1, :], ALU.subtract).then_inc(had_add, 1)

            def w2_scale():
                dve.wait_ge(had_add, 3)
                dve.tensor_scalar(w2b, w2a, 1.0 / np.sqrt(FF), None, ALU.mult).then_inc(had_add, 1)

            def w2_high():
                dve.wait_ge(had_add, 4)
                dve.tensor_copy(w2h[0], w2b).then_inc(w2_ready, 1)

            def w2_low():
                dve.wait_ge(w2_ready, 1)
                dve.tensor_tensor(w2h[1], w2b, w2h[0].bitcast(F32), ALU.subtract).then_inc(w2_ready, 1)

            h_lows(0)
            start_at_one(dve, ff_add)
            x1_lows(1)
            hidden(0, True, [lambda n=n: butterflies(n) for n in range(3)] + [w2_scale, w2_high, w2_low])
            xa_lows(1, BC)
            h_lows(1)
            add_x1(0, 0, True)
            with dve.Fori(1, NCH - 1) as c:
                x1_lows(c + 1)
                hidden(c, False)
                xa_lows(c + 1, c * BC + BC)
                h_lows(c + 1)
                add_x1(c, c * QC, False)
            hidden(NCH - 1, False)
            add_x1(NCH - 1, (NCH - 1) * QC, False)


def kernel(x, itok_B_1_198, itok_B_0_6, L0_cond_weights, L0_attn_W_qkv, L0_attn_W_z, L0_attn_W_b, L0_attn_W_a,
           L0_attn_conv_w, L0_attn_dt_bias, L0_attn_A_log, L0_attn_norm_w, L0_attn_W_out, L0_cond2_W, L0_cond2_A,
           L0_cond2_Bm, L0_cond2_scalings, L0_ffn_W1, L0_ffn_W2, L0_ffn_W3):
    import concourse.bacc as _bacc
    from concourse.bass_utils import run_bass_kernel_spmd as _run

    c = np.ascontiguousarray

    def tiles(w):
        return np.asarray(w).reshape(-1, HD, KH, P).transpose(0, 3, 2, 1)

    wqkv = tiles(L0_attn_W_qkv)
    wz = tiles(L0_attn_W_z)
    taps = np.asarray(L0_attn_conv_w).reshape(-1, HD, TAPS)
    kdim = NKH
    qk = np.concatenate([wqkv[0:kdim].reshape(NKH, P, -1), wqkv[kdim:2 * kdim].reshape(NKH, P, -1),
                         taps[0:kdim], taps[kdim:2 * kdim]], axis=2)
    wv = wqkv[2 * kdim:].reshape(NKH, NV, P, KH * HD)
    wzz = wz.reshape(NKH, NV, P, KH * HD)
    tv = taps[2 * kdim:].reshape(NKH, NV, HD, TAPS)
    vz = np.concatenate([wv[:, 0], wzz[:, 0], wv[:, 1], wzz[:, 1], tv[:, 0], tv[:, 1]], axis=2)
    wo = np.asarray(L0_attn_W_out).T.reshape(NKH, NV, HD, HID).transpose(0, 2, 1, 3).reshape(NKH, HD, NV * HID)
    wab = np.zeros((P, KH, P), np.float32)
    wab[:, :, 0:NVH] = np.asarray(L0_attn_W_a).T.reshape(KH, P, NVH).transpose(1, 0, 2)
    wab[:, :, NVH:2 * NVH] = np.asarray(L0_attn_W_b).T.reshape(KH, P, NVH).transpose(1, 0, 2)
    gcol = np.zeros((2 * NVH, 2), np.float32)
    gcol[0:NVH, 0] = np.asarray(L0_attn_dt_bias)
    gcol[0:NVH, 1] = np.asarray(L0_attn_A_log)
    had = np.ones((1, 1), np.float32)
    while had.shape[0] < P:
        had = np.block([[had, had], [had, -had]])
    rows_of = lambda w, n: np.asarray(w).T.reshape(n, P, -1).transpose(1, 0, 2)
    ins = {
        "x": np.asarray(x),
        "itok_set": np.asarray(itok_B_1_198).reshape(B, 1),
        "itok_ad": np.asarray(itok_B_0_6).reshape(B),
        "cond_w": np.asarray(L0_cond_weights).reshape(NSETS, T * T),
        "w_qk": qk, "w_vz": vz, "w_o": wo, "w_ab": wab, "gate_col": gcol,
        "norm_w": np.asarray(L0_attn_norm_w).reshape(HD, 1),
        "lora_w": rows_of(L0_cond2_W, KH),
        "lora_a": rows_of(np.asarray(L0_cond2_A).reshape(NAD * RANK, HID), KH),
        "lora_b": np.asarray(L0_cond2_Bm).transpose(0, 2, 1).reshape(NAD * RANK, HID),
        "scal_col": np.repeat(np.asarray(L0_cond2_scalings), RANK).reshape(P, 1),
        "ad_col": np.repeat(np.arange(NAD, dtype=np.float32), RANK).reshape(P, 1),
        "w1": rows_of(L0_ffn_W1, KH), "w3": rows_of(L0_ffn_W3, KH), "w2": rows_of(L0_ffn_W2, FT),
        "had": had, "ident_in": np.eye(P, dtype=np.float32),
    }
    nc = _bacc.Bacc("TRN2", target_bir_lowering=False, num_devices=1)
    arrays, args = {}, []
    for name, a in ins.items():
        a = c(a)
        arrays[f"in_{name}"] = a
        args.append(nc.dram_tensor(f"in_{name}", a.shape, mybir.dt.from_np(a.dtype), kind="ExternalInput").ap())
    args.append(nc.dram_tensor("out_0", (B, T, HID), F32, kind="ExternalOutput").ap())
    build_program(nc, *args)
    r = _run(nc, [arrays], core_ids=[0])
    return r.results[0]["out_0"]
```
